# Optimizing a Trainium2 kernel written in Bass

```python
import numpy as np
import jax
import jax.numpy as jnp

def _softmax(x, axis=-1):
    return jax.nn.softmax(x, axis=axis)

def _gelu(x):
    return jax.nn.gelu(x, approximate=True)

def _silu(x):
    return jax.nn.silu(x)

def _sigmoid(x):
    return jax.nn.sigmoid(x)

def _layernorm(x, axis=-1, eps=1e-05):
    m = jnp.mean(x, axis=axis, keepdims=True)
    v = jnp.var(x, axis=axis, keepdims=True)
    return (x - m) / jnp.sqrt(v + eps)

def _scatter_add(tgt, idx, src, axis=0):
    return tgt.at[idx].add(src)

def _segment_sum(src, seg, n):
    return jax.ops.segment_sum(src, seg, n)
kernel_name = 'mk_prb_d1_jaxref_r4_ff54b8'

def setup_inputs(seed: int=0):
    np.random.seed(seed)
    _w = jnp.asarray

    def _L0_attn_setup():
        import jax, jax.numpy as jnp
        import numpy as np
        D_OUT = 256
        key = jax.random.key(seed)
        k1, k2 = jax.random.split(key)
        x = jax.random.normal(k1, (4, 512, 256), dtype=jnp.float32)
        W_qkv = jax.random.normal(k2, (256, 3 * D_OUT), dtype=jnp.float32) * 0.02
        return {'x': x, 'W_qkv': W_qkv}
    _L0_attn_in = _L0_attn_setup()

    def _L0_ffn_setup():
        import jax, jax.numpy as jnp
        import numpy as np
        H = 256
        I = 512
        E = 32
        B, S = (4, 512)

        def _grouped_mm(a, w, group_sizes):
            return jax.lax.ragged_dot(a, w, group_sizes)

        def _swiglu(x, gw, uw, dw):
            return jax.nn.silu(x @ gw) * (x @ uw) @ dw
        key = jax.random.key(seed)
        ks = jax.random.split(key, 8)
        scale = 0.02
        inp = {'hidden_states': jax.random.normal(ks[0], (B, S, H), dtype=jnp.float32), 'gate_w': jax.random.normal(ks[1], (H, E), dtype=jnp.float32) * scale, 'shared_gate_w': jax.random.normal(ks[2], (H, I), dtype=jnp.float32) * scale, 'shared_up_w': jax.random.normal(ks[3], (H, I), dtype=jnp.float32) * scale, 'shared_down_w': jax.random.normal(ks[4], (I, H), dtype=jnp.float32) * scale, 'routed_gate_w': jax.random.normal(ks[5], (E, H, I), dtype=jnp.float32) * scale, 'routed_up_w': jax.random.normal(ks[6], (E, H, I), dtype=jnp.float32) * scale, 'routed_down_w': jax.random.normal(ks[7], (E, I, H), dtype=jnp.float32) * scale}
        return inp
    _L0_ffn_in = _L0_ffn_setup()
    _d = {'L0_attn_x': _L0_attn_in['x'], 'L0_attn_W_qkv': _L0_attn_in['W_qkv'], 'L0_ffn_gate_w': _L0_ffn_in['gate_w'], 'L0_ffn_shared_gate_w': _L0_ffn_in['shared_gate_w'], 'L0_ffn_shared_up_w': _L0_ffn_in['shared_up_w'], 'L0_ffn_shared_down_w': _L0_ffn_in['shared_down_w'], 'L0_ffn_routed_gate_w': _L0_ffn_in['routed_gate_w'], 'L0_ffn_routed_up_w': _L0_ffn_in['routed_up_w'], 'L0_ffn_routed_down_w': _L0_ffn_in['routed_down_w']}
    _x0 = _d['L0_attn_x']
    _d['L0_attn_x'] = jax.random.normal(jax.random.fold_in(jax.random.key(seed), 1), (8, 2048, 256), dtype=_x0.dtype)
    del _x0
    return _d

def reference(L0_attn_x, L0_attn_W_qkv, L0_ffn_gate_w, L0_ffn_shared_gate_w, L0_ffn_shared_up_w, L0_ffn_shared_down_w, L0_ffn_routed_gate_w, L0_ffn_routed_up_w, L0_ffn_routed_down_w):

    def _L0_attn_ref(x, W_qkv):
        import jax, jax.numpy as jnp
        import numpy as np
        D_OUT = 256
        B, N, _ = x.shape
        scale = D_OUT ** 0.5
        qkv = jnp.einsum('bnd,de->bne', x, W_qkv)
        q, k, v = jnp.split(qkv, 3, axis=-1)
        scores = jnp.einsum('bnd,bmd->bnm', q, k) / scale
        causal = jnp.triu(jnp.ones((N, N), dtype=bool), k=1)
        scores = jnp.where(causal, -jnp.inf, scores)
        attn = jax.nn.softmax(scores, axis=-1)
        return jnp.einsum('bnm,bmd->bnd', attn, v)

    def _L0_ffn_ref(hidden_states, gate_w, shared_gate_w, shared_up_w, shared_down_w, routed_gate_w, routed_up_w, routed_down_w):
        import jax, jax.numpy as jnp
        import numpy as np
        H = 256
        I = 512
        E = 32
        B, S = (4, 512)

        def _grouped_mm(a, w, group_sizes):
            return jax.lax.ragged_dot(a, w, group_sizes)

        def _swiglu(x, gw, uw, dw):
            return jax.nn.silu(x @ gw) * (x @ uw) @ dw
        b, s, h = hidden_states.shape
        x = hidden_states.reshape(-1, h)
        shared_out = _swiglu(x, shared_gate_w, shared_up_w, shared_down_w)
        logits = x @ gate_w
        topk_ids = jnp.argmax(logits, axis=-1)
        topk_val = jnp.max(logits, axis=-1)
        scores = jax.nn.sigmoid(topk_val)[:, None]
        xs = x * scores
        tokens_per_expert = jnp.zeros((E,), jnp.int32).at[topk_ids].add(1)
        order = jnp.argsort(topk_ids)
        sorted_x = xs[order]
        g = _grouped_mm(sorted_x, routed_gate_w, tokens_per_expert)
        u = _grouped_mm(sorted_x, routed_up_w, tokens_per_expert)
        d = _grouped_mm(jax.nn.silu(g) * u, routed_down_w, tokens_per_expert)
        inv = jnp.argsort(order)
        routed_out = d[inv]
        return (shared_out + routed_out).reshape(b, s, h)
    x = L0_attn_x
    xn = _layernorm(x, axis=-1)
    x = x + _L0_attn_ref(xn, L0_attn_W_qkv) + _L0_ffn_ref(xn, L0_ffn_gate_w, L0_ffn_shared_gate_w, L0_ffn_shared_up_w, L0_ffn_shared_down_w, L0_ffn_routed_gate_w, L0_ffn_routed_up_w, L0_ffn_routed_down_w)
    return x

_drawn_inputs = setup_inputs


def setup_inputs(seed=0):
    import zlib

    import numpy as np

    out = dict(_drawn_inputs(seed))
    spreads = {}
    factors = {'L0_attn_W_qkv': 9.117,
     'L0_ffn_gate_w': 5.569,
     'L0_ffn_routed_gate_w': 5.507,
     'L0_ffn_routed_up_w': 5.48,
     'L0_ffn_routed_down_w': 5.484,
     'L0_ffn_shared_gate_w': 8.0,
     'L0_ffn_shared_up_w': 8.0,
     'L0_ffn_shared_down_w': 8.0}
    for name, (base, spread) in spreads.items():
        noise = np.random.default_rng([zlib.crc32(name.encode()), seed]).standard_normal(out[name].shape)
        drawn = base * np.exp(spread * noise) if base else spread * noise
        out[name] = jnp.asarray(drawn.astype(out[name].dtype))
    for name, factor in factors.items():
        out[name] = (out[name] * factor).astype(out[name].dtype)
    return out
```

```python
from contextlib import ExitStack

import concourse.bass as bass
from concourse import mybir

F32 = mybir.dt.float32
F32R = mybir.dt.float32r
BF16 = mybir.dt.bfloat16
I32 = mybir.dt.int32
U32 = mybir.dt.uint32
ALU = mybir.AluOpType
ACT = mybir.ActivationFunctionType
AX = mybir.AxisListType

P = 128
EPS = 1e-5
EULER = 2.718281828459045
MASKED = -1e30
GT = 512
ST = 256


def wait(eng, sem, value):
    if isinstance(value, int) and value <= 0:
        return
    eng.wait_ge(sem, value)


def is_first(g):
    return isinstance(g, int) and g == 0


def wait_apart(eng, sem, value, passed):
    if isinstance(value, int) and value <= 0:
        return
    eng.wait_ge(sem, value)
    eng.sem_inc(passed, 1)


def each_pair(eng, n, body):
    for i in range(min(2, n - 1)):
        body(i, False)
    if n > 3:
        with eng.Fori(2, n - 1) as i:
            body(i, False)
    body(n - 1, True)


def setup_stage(nc, ctx, W_qkv, keep, D):
    C = D // P
    with ExitStack() as st:
        wqkv = st.enter_context(nc.sbuf_tensor("wqkv", [P, C, 3 * D], F32))
        wT = st.enter_context(nc.sbuf_tensor("wT", [P, 2, C, D], F32))
        a32 = st.enter_context(nc.sbuf_tensor("a32", [P, C, D], F32))
        maskf = st.enter_context(nc.sbuf_tensor("maskf", [P, P], F32))
        psT = st.enter_context(nc.psum_tensor("psT", [P, 4, 2 * D], F32))
        psA = st.enter_context(nc.psum_tensor("psA", [P, C, 2 * D], F32))
        w_in, zeroed, ident_ok, wt_mm, wt_ok, a_mm, a_ok, hi_ok, done = (
            st.enter_context(nc.semaphore(n)) for n in
            ("w_in", "zeroed", "ident_ok", "wt_mm", "wt_ok", "a_mm", "a_ok", "whi_ok", "setup_done"))
        block = st.enter_context(nc.Block())

        @block.sync
        def _(sp):
            sp.dma_start(wqkv[:], W_qkv.rearrange("(c p) n -> p c n", p=P)).then_inc(w_in, 16)

        @block.gpsimd
        def _(pool):
            g = nc.gpsimd
            g.memset(keep.ident[:], 0.0).then_inc(zeroed, 1)
            g.memset(maskf[:], 0.0).then_inc(zeroed, 1)
            g.memset(keep.neghalf[:], -0.5)
            g.memset(keep.euler[:], EULER)
            pool.wait_ge(zeroed, 2)
            g.affine_select(out=keep.ident[:], in_=keep.ident[:], compare_op=ALU.not_equal, fill=1.0,
                            base=0, pattern=[[-1, P]], channel_multiplier=1).then_inc(ident_ok, 1)
            g.affine_select(out=maskf[:], in_=maskf[:], compare_op=ALU.is_ge, fill=MASKED,
                            base=0, pattern=[[-1, P]], channel_multiplier=1).then_inc(ident_ok, 1)

        @block.tensor
        def _(pe):
            pe.wait_ge(w_in, 16)
            pe.wait_ge(ident_ok, 1)
            for w in range(2):
                for e in range(C):
                    for c in range(C):
                        mm = nc.tensor.transpose(psT[:, w * C + e, c * P:(c + 1) * P],
                                                 wqkv[:, c, w * D + e * P:w * D + (e + 1) * P], keep.ident[:])
            mm.then_inc(wt_mm, 1)
            pe.wait_ge(wt_ok, 1)
            for c in range(C):
                for e in range(C):
                    mm = nc.tensor.matmul(psA[:, c, 0:D], wT[:, 0, e, c * P:(c + 1) * P], wT[:, 1, e, :],
                                          start=(e == 0), stop=(e == C - 1))
            mm.then_inc(a_mm, 1)

        @block.scalar
        def _(act):
            act.wait_ge(w_in, 16)
            nc.scalar.copy(keep.v_hi[:], wqkv[:, :, 2 * D:3 * D]).then_inc(hi_ok, 1)
            act.wait_ge(a_ok, 1)
            nc.scalar.copy(keep.a_hi[:], a32[:]).then_inc(hi_ok, 1)

        @block.vector
        def _(dve):
            v = nc.vector
            dve.wait_ge(ident_ok, 2)
            v.tensor_copy(keep.ident_bf[:], keep.ident[:])
            v.tensor_copy(keep.mask_bf[:], maskf[:])
            dve.wait_ge(wt_mm, 1)
            v.tensor_copy(wT[:].rearrange("p w e d -> p (w e) d"), psT[:, :, 0:D]).then_inc(wt_ok, 1)
            dve.wait_ge(a_mm, 1)
            v.tensor_scalar(a32[:], psA[:, :, 0:D], float(D) ** -0.5, None, ALU.mult).then_inc(a_ok, 1)
            dve.wait_ge(hi_ok, 1)
            v.tensor_tensor(keep.v_lo[:], wqkv[:, :, 2 * D:3 * D], keep.v_hi[:].bitcast(F32), ALU.subtract)
            dve.wait_ge(hi_ok, 2)
            dve.wait_ge(a_ok, 1)
            v.tensor_tensor(keep.a_lo[:], a32[:], keep.a_hi[:].bitcast(F32), ALU.subtract)


def split_matmuls(nc, out, hi, lo, rhi, rlo, first, last):
    nc.tensor.matmul(out, hi, rhi, start=first, stop=False, skip_group_check=True)
    nc.tensor.matmul(out, lo, rhi, start=False, stop=False, skip_group_check=True)
    return nc.tensor.matmul(out, hi, rlo, start=False, stop=last, skip_group_check=True)


def token_stage(nc, x_g, gate_w, sgw, suw, sdw, xs_g, xth_g, xtl_g, sh_g, keep, D, F, E, NG):
    C, J, IT = D // P, GT // P, F // P
    with ExitStack() as st:
        def sb(name, shape, dt=F32):
            return st.enter_context(nc.sbuf_tensor("a_" + name, shape, dt))

        def ps(name, shape):
            return st.enter_context(nc.psum_tensor("a_" + name, shape, F32))

        def sem(name):
            return st.enter_context(nc.semaphore("a_" + name))

        wraw = sb("wraw", [P, 3, IT * D])
        raw = [wraw[:, 0].rearrange("p (c f) -> p c f", c=C), wraw[:, 1].rearrange("p (c f) -> p c f", c=C),
               wraw[:, 2].rearrange("p (i d) -> p i d", i=IT)]
        w_hi = [sb("gw_hi", [P, C, F], F32R), sb("uw_hi", [P, C, F], F32R), sb("dw_hi", [P, IT, D], F32R)]
        w_lo = [sb("gw_lo", [P, C, F], F32R), sb("uw_lo", [P, C, F], F32R), sb("dw_lo", [P, IT, D], F32R)]
        gate = sb("gate", [P, C, E])
        gate_hl = sb("gate_hl", [P, C, 2, E], F32R)
        xt = sb("xt", [P, 2, J, D])
        stats = sb("stats", [P, 2, J, 6])
        mv = sb("mv", [P, 2, J, 2])
        ve = sb("ve", [P, 2, J])
        rstd = sb("rstd", [P, 2, J])
        xn = sb("xn", [P, 2, J, D])
        xT_hi = [sb(f"xT_hi{k}", [P, C, GT], F32R) for k in range(2)]
        xT_lo = [sb(f"xT_lo{k}", [P, C, GT], F32R) for k in range(2)]
        silu = sb("silu", [P, 2, GT])
        h32 = sb("h32", [P, IT, GT])
        h_hi = [sb(f"h_hi{k}", [P, IT, GT], F32R) for k in range(2)]
        h_lo = [sb(f"h_lo{k}", [P, IT, GT], F32R) for k in range(2)]
        sh = sb("sh", [P, 2, J, D])
        lg2 = sb("lg2", [P, J, 2, E])
        lg = sb("lg", [P, J, E])
        top = sb("top", [P, J, 8])
        topi = sb("topi", [P, J, 8], U32)
        negtop = sb("negtop", [P, J])
        eneg = sb("eneg", [P, J])
        score = sb("score", [P, 2, J])
        xs = sb("xs", [P, 2, J, D])
        psT = ps("psT", [P, 2, 512])
        psG = ps("psG", [P, 2, 512])
        psU = ps("psU", [P, 2, 512])
        psD = ps("psD", [P, J, D])
        psL = psT[:, 0, 0:J * 2 * E].rearrange("p (j n) -> p j n", j=J)

        w_in, gate_in, w_hi_ok, w_ok, gate_ok = (sem(n) for n in ("w_in", "gate_in", "w_hi_ok", "w_ok", "gate_ok"))
        x_in = [sem(f"x_in{k}") for k in range(2)]
        xs_out = [sem(f"xs_out{k}") for k in range(2)]
        xt_out = [sem(f"xt_out{k}") for k in range(2)]
        sh_out = [sem(f"sh_out{k}") for k in range(2)]
        var_ok, rstd_ok, xn_ok, t_mm, xh_ok, xl_ok = (sem(n) for n in ("var_ok", "rstd_ok", "xn_ok", "t_mm", "xh_ok", "xl_ok"))
        g_mm, u_mm, silu_ok, h_ok, hhi_ok, hlo_ok, d_mm, sh_ok = (
            sem(n) for n in ("g_mm", "u_mm", "silu_ok", "h_ok", "hhi_ok", "hlo_ok", "d_mm", "sh_ok"))
        lg_mm, lg_ok, ntop_ok, eneg_ok, xs_ok, rt_step = (
            sem(n) for n in ("lg_mm", "lg_ok", "ntop_ok", "eneg_ok", "xs_ok", "rt_step"))
        ln_step, passed = sem("ln_step"), sem("passed")
        block = st.enter_context(nc.Block())

        @block.sync
        def _(sp):
            sp.dma_start(gate[:], gate_w.rearrange("(c p) e -> p c e", p=P)).then_inc(gate_in, 16)
            for k in range(2):
                sp.dma_start(xt[:, k], x_g[k]).then_inc(x_in[k], 16)
            sp.dma_start(raw[0], sgw.rearrange("(c p) f -> p c f", p=P)).then_inc(w_in, 16)
            sp.dma_start(raw[1], suw.rearrange("(c p) f -> p c f", p=P)).then_inc(w_in, 16)
            sp.dma_start(raw[2], sdw.rearrange("(i p) d -> p i d", p=P)).then_inc(w_in, 16)

            def store_xt(g, k):
                wait(sp, xh_ok, C * (g + 1))
                sp.dma_start(xth_g[g], xT_hi[k][:].bitcast(F32)).then_inc(xt_out[k], 16)
                wait(sp, xl_ok, C * (g + 1))
                sp.dma_start(xtl_g[g], xT_lo[k][:].bitcast(F32)).then_inc(xt_out[k], 16)
                wait(sp, xs_ok, g + 1)
                sp.dma_start(xs_g[g], xs[:, k]).then_inc(xs_out[k], 16)

            def store_sh(g, k):
                wait(sp, sh_ok, g + 1)
                sp.dma_start(sh_g[g], sh[:, k]).then_inc(sh_out[k], 16)

            store_xt(0, 0)

            def pair(i, last):
                for k in range(2):
                    g = 2 * i + k
                    if not last:
                        wait(sp, xn_ok, g + 1)
                        sp.dma_start(xt[:, k], x_g[g + 2]).then_inc(x_in[k], 16)
                    if not (last and k == 1):
                        store_xt(g + 1, 1 - k)
                    if not is_first(g):
                        store_sh(g - 1, 1 - k)
            each_pair(sp, NG // 2, pair)
            store_sh(NG - 1, 1)
            for k in range(2):
                sp.wait_ge(xt_out[k], 32 * (NG // 2))
                sp.wait_ge(xs_out[k], 16 * (NG // 2))
                sp.wait_ge(sh_out[k], 16 * (NG // 2))

        @block.gpsimd
        def _(pool):
            def rstd_of(g, k):
                wait(pool, var_ok, g + 1)
                nc.gpsimd.tensor_tensor(rstd[:, k], ve[:, k], keep.neghalf[:], ALU.pow).then_inc(rstd_ok, 1)

            def eneg_of(g):
                wait(pool, ntop_ok, g + 1)
                nc.gpsimd.tensor_tensor(eneg[:], keep.euler[:], negtop[:], ALU.pow).then_inc(eneg_ok, 1)

            rstd_of(0, 0)
            eneg_of(0)
            rstd_of(1, 1)

            def pair(i, last):
                for k in range(2):
                    g = 2 * i + k
                    if not (last and k == 1):
                        eneg_of(g + 1)
                    if not last:
                        rstd_of(g + 2, k)
            each_pair(pool, NG // 2, pair)

        @block.vector
        def _(dve):
            v = nc.vector
            dve.wait_ge(gate_in, 16)
            v.tensor_copy(gate_hl[:, :, 0], gate[:]).then_inc(gate_ok, 1)
            dve.wait_ge(gate_ok, 1)
            v.tensor_tensor(gate_hl[:, :, 1], gate[:], gate_hl[:, :, 0].bitcast(F32), ALU.subtract).then_inc(gate_ok, 1)

            def stats_of(g, k, i):
                wait(dve, x_in[k], 16 * (i + 1))
                for j in range(J):
                    s = v.bn_stats(stats[:, k, j], xt[:, k, j])
                s.then_inc(ln_step, 1)
                wait_apart(dve, ln_step, 2 * g + 1, passed)
                for j in range(J):
                    s = v.bn_aggr(mv[:, k, j], stats[:, k, j])
                s.then_inc(ln_step, 1)
                wait(dve, ln_step, 2 * g + 2)
                v.tensor_scalar(ve[:, k], mv[:, k, :, 1], EPS, None, ALU.add).then_inc(var_ok, 1)

            def norm(g, k):
                wait(dve, rstd_ok, g + 1)
                for j in range(J):
                    s = v.tensor_scalar(xn[:, k, j], xt[:, k, j], mv[:, k, j, 0:1], rstd[:, k, j:j + 1],
                                        ALU.subtract, ALU.mult)
                s.then_inc(xn_ok, 1)

            def xT_low(g, k, i):
                wait(dve, xt_out[k], 32 * i)
                for c in range(C):
                    wait(dve, xh_ok, C * g + c + 1)
                    v.tensor_tensor(xT_lo[k][:, c], psT[:, c], xT_hi[k][:, c].bitcast(F32), ALU.subtract).then_inc(xl_ok, 1)

            def route(g, k, i):
                wait(dve, lg_ok, g + 1)
                wait(dve, xn_ok, g + 1)
                n = 5 * g
                v.tensor_tensor(lg[:], lg2[:, :, 0], lg2[:, :, 1], ALU.add).then_inc(rt_step, 1)
                wait_apart(dve, rt_step, n + 1, passed)
                for j in range(J):
                    s = v.max(top[:, j], lg[:, j])
                s.then_inc(rt_step, 1)
                wait(dve, rt_step, n + 2)
                v.tensor_scalar(negtop[:], top[:, :, 0], -1.0, None, ALU.mult).then_inc(ntop_ok, 1)
                for j in range(J):
                    s = v.max_index(topi[:, j], top[:, j], lg[:, j])
                s.then_inc(rt_step, 1)
                wait(dve, rt_step, n + 3)
                v.tensor_copy(keep.expert[:, bass.ds(g * J, J)], topi[:, :, 0])
                wait(dve, eneg_ok, g + 1)
                v.tensor_scalar(eneg[:], eneg[:], 1.0, None, ALU.add).then_inc(rt_step, 1)
                wait(dve, rt_step, n + 4)
                v.reciprocal(score[:, k], eneg[:]).then_inc(rt_step, 1)
                wait(dve, rt_step, n + 5)
                wait(dve, xs_out[k], 16 * i)
                for j in range(J):
                    s = v.tensor_scalar(xs[:, k, j], xn[:, k, j], score[:, k, j:j + 1], None, ALU.mult)
                s.then_inc(xs_ok, 1)

            def mul(g, it):
                wait(dve, u_mm, IT * g + it + 1)
                wait(dve, silu_ok, IT * g + it + 1)
                wait(dve, hlo_ok, IT * (g - 1) + it + 1)
                v.tensor_tensor(h32[:, it], silu[:, it % 2], psU[:, it % 2], ALU.mult).then_inc(h_ok, 1)

            def h_low(g, k, it):
                wait(dve, hhi_ok, IT * g + it + 1)
                v.tensor_tensor(h_lo[k][:, it], h32[:, it], h_hi[k][:, it].bitcast(F32), ALU.subtract).then_inc(hlo_ok, 1)

            stats_of(0, 0, 0)
            norm(0, 0)
            for n in range(3):
                dve.wait_ge(w_hi_ok, n + 1)
                v.tensor_tensor(w_lo[n][:], raw[n], w_hi[n][:].bitcast(F32), ALU.subtract).then_inc(w_ok, 1)
            xT_low(0, 0, 0)
            route(0, 0, 0)
            stats_of(1, 1, 0)
            norm(1, 1)

            def pair(i, last):
                for k in range(2):
                    g = 2 * i + k
                    mul(g, 0)
                    mul(g, 1)
                    h_low(g, k, 0)
                    mul(g, 2)
                    h_low(g, k, 1)
                    mul(g, 3)
                    h_low(g, k, 2)
                    if not (last and k == 1):
                        xT_low(g + 1, 1 - k, i + k)
                    h_low(g, k, 3)
                    if not (last and k == 1):
                        route(g + 1, 1 - k, i + k)
                    if not last:
                        stats_of(g + 2, k, i + 1)
                        norm(g + 2, k)
            each_pair(dve, NG // 2, pair)

        @block.scalar
        def _(act):
            s = nc.scalar

            def xT_high(g, k, i):
                wait(act, xt_out[k], 32 * i)
                wait(act, u_mm, IT * (g - 1))
                for c in range(C):
                    wait(act, t_mm, C * g + c + 1)
                    s.copy(xT_hi[k][:, c], psT[:, c]).then_inc(xh_ok, 1)

            def logits(g):
                wait(act, lg_mm, g + 1)
                s.copy(lg2[:].rearrange("p j a e -> p j (a e)"), psL).then_inc(lg_ok, 1)

            def silu_of(g, it):
                wait(act, g_mm, IT * g + it + 1)
                wait(act, h_ok, IT * g + it - 1)
                s.activation(silu[:, it % 2], psG[:, it % 2], ACT.Silu).then_inc(silu_ok, 1)

            def h_high(g, k, it):
                wait(act, h_ok, IT * g + it + 1)
                wait(act, d_mm, g - 1)
                s.copy(h_hi[k][:, it], h32[:, it]).then_inc(hhi_ok, 1)

            def shared_out(g, k, i):
                wait(act, d_mm, g + 1)
                wait(act, sh_out[k], 16 * i)
                s.copy(sh[:, k], psD[:]).then_inc(sh_ok, 1)

            act.wait_ge(w_in, 48)
            for n in range(3):
                s.copy(w_hi[n][:], raw[n]).then_inc(w_hi_ok, 1)
            xT_high(0, 0, 0)
            logits(0)

            def pair(i, last):
                for k in range(2):
                    g = 2 * i + k
                    silu_of(g, 0)
                    silu_of(g, 1)
                    h_high(g, k, 0)
                    silu_of(g, 2)
                    h_high(g, k, 1)
                    silu_of(g, 3)
                    h_high(g, k, 2)
                    if not (last and k == 1):
                        xT_high(g + 1, 1 - k, i + k)
                    h_high(g, k, 3)
                    if not is_first(g):
                        shared_out(g - 1, 1 - k, i - 1 + k)
                    if not (last and k == 1):
                        logits(g + 1)
            each_pair(act, NG // 2, pair)
            shared_out(NG - 1, 1, NG // 2 - 1)

        @block.tensor
        def _(pe):
            def transposes(g, k):
                wait(pe, xn_ok, g + 1)
                wait(pe, lg_ok, g)
                wait(pe, xl_ok, C * g)
                for c in range(C):
                    for j in range(J):
                        mm = nc.tensor.transpose(psT[:, c, j * P:(j + 1) * P],
                                                 xn[:, k, j, c * P:(c + 1) * P], keep.ident[:])
                    mm.then_inc(t_mm, 1)

            def logits(g, k):
                wait(pe, xl_ok, C * (g + 1))
                for j in range(J):
                    for c in range(C):
                        nc.tensor.matmul(psL[:, j], xT_hi[k][:, c, j * P:(j + 1) * P],
                                         gate_hl[:, c].rearrange("p a e -> p (a e)"),
                                         start=(j == 0 and c == 0), stop=False, skip_group_check=True)
                    for c in range(C):
                        mm = nc.tensor.matmul(psL[:, j, 0:E], xT_lo[k][:, c, j * P:(j + 1) * P], gate_hl[:, c, 0],
                                              start=False, stop=(c == C - 1), skip_group_check=True)
                mm.then_inc(lg_mm, 1)

            def up(g, k):
                wait(pe, xl_ok, C * (g + 1))
                for it in range(IT):
                    cols = slice(it * P, (it + 1) * P)
                    wait(pe, silu_ok, IT * g + it - 1)
                    for c in range(C):
                        mm = split_matmuls(nc, psG[:, it % 2], w_hi[0][:, c, cols], w_lo[0][:, c, cols],
                                           xT_hi[k][:, c], xT_lo[k][:, c], c == 0, c == C - 1)
                    mm.then_inc(g_mm, 1)
                    wait(pe, h_ok, IT * g + it - 1)
                    for c in range(C):
                        mm = split_matmuls(nc, psU[:, it % 2], w_hi[1][:, c, cols], w_lo[1][:, c, cols],
                                           xT_hi[k][:, c], xT_lo[k][:, c], c == 0, c == C - 1)
                    mm.then_inc(u_mm, 1)

            def down(g, k):
                wait(pe, sh_ok, g)
                for it in range(IT):
                    wait(pe, hlo_ok, IT * g + it + 1)
                    for j in range(J):
                        cols = slice(j * P, (j + 1) * P)
                        mm = split_matmuls(nc, psD[:, j], h_hi[k][:, it, cols], h_lo[k][:, it, cols],
                                           w_hi[2][:, it], w_lo[2][:, it],
                                           it == 0 and j % 2 == 0, it == IT - 1)
                mm.then_inc(d_mm, 1)

            pe.wait_ge(gate_ok, 2)
            transposes(0, 0)
            logits(0, 0)
            pe.wait_ge(w_ok, 3)

            def pair(i, last):
                for k in range(2):
                    g = 2 * i + k
                    up(g, k)
                    if not (last and k == 1):
                        transposes(g + 1, 1 - k)
                    if not is_first(g):
                        down(g - 1, 1 - k)
                    if not (last and k == 1):
                        logits(g + 1, 1 - k)
            each_pair(pe, NG // 2, pair)
            down(NG - 1, 1)


def routing_stage(nc, keep, E, NT, ET):
    NC = ET * ST // P
    with ExitStack() as st:
        def sb(name, shape, dt=F32):
            return st.enter_context(nc.sbuf_tensor("r_" + name, shape, dt))

        def sem(name):
            return st.enter_context(nc.semaphore("r_" + name))

        one_hot = sb("one_hot", [P, E, NT])
        zeros = sb("zeros", [P, E * NT])
        cum = sb("cum", [P, E, NT])
        ends = sb("ends", [P, E + 1])
        here = sb("here", [P, E])
        counts = sb("counts", [P, 2, E])
        tiles_i = sb("tiles_i", [P, E], I32)
        tiles_s = sb("tiles_s", [P, E], I32)
        tiles = sb("tiles", [P, E])
        tiles_cum = sb("tiles_cum", [P, E])
        base = sb("base", [P, E])
        shift = sb("shift", [P, E])
        pos = sb("pos", [P, NT])
        pos_i = sb("pos_i", [P, NT], I32)
        lo_i = sb("lo_i", [P, NT], I32)
        hi_i = sb("hi_i", [P, NT], I32)
        lo = sb("lo", [P, NT])
        hi = sb("hi", [P, NT])
        col_i = sb("col_i", [P, max(NC, P, NT)], I32)
        row_i = sb("row_i", [P, 1], I32)
        col = sb("col", [P, max(NC, P, NT)])
        col_bf = sb("col_bf", [P, max(NC, P)], BF16)
        row = sb("row", [P, 1])
        below = sb("below", [P, P])
        ones = sb("ones", [P, P])
        lo_hot = sb("lo_hot", [P, 2, P], BF16)
        hi_hot = sb("hi_hot", [P, 2, 2, NC], BF16)
        past = sb("past", [1, ET, E])
        tile_f = sb("tile_f", [1, ET])
        slot_t = sb("slot_t", [P, NC])
        slot_f = sb("slot_f", [P, NC])
        psC = st.enter_context(nc.psum_tensor("r_psC", [P, 2, E], F32))
        psS = st.enter_context(nc.psum_tensor("r_psS", [P, 2, NC], F32))
        consts, hot_ok, here_ok, c_mm, step, loop_ok, s_mm = (
            sem(n) for n in ("consts", "hot_ok", "here_ok", "c_mm", "step", "loop_ok", "s_mm"))
        block = st.enter_context(nc.Block())

        @block.gpsimd
        def _(pool):
            g = nc.gpsimd
            g.iota(col_i[:], pattern=[[1, col_i.shape[1]]], base=0, channel_multiplier=0).then_inc(consts, 1)
            g.iota(row_i[:], pattern=[[1, 1]], base=0, channel_multiplier=1).then_inc(consts, 1)
            g.memset(ones[:], 1.0).then_inc(consts, 1)
            pool.wait_ge(consts, 3)
            g.affine_select(out=below[:], in_=ones[:], compare_op=ALU.is_gt, fill=0.0,
                            base=0, pattern=[[1, P]], channel_multiplier=-1).then_inc(consts, 1)

        @block.vector
        def _(dve):
            v = nc.vector
            n = [0]

            def done(ins):
                n[0] += 1
                ins.then_inc(step, 1)
                dve.wait_ge(step, n[0])

            v.memset(zeros[:], 0.0)
            v.memset(ends[:, 0:1], 0.0)
            for e in range(E):
                h = v.tensor_scalar(one_hot[:, e], keep.expert[:], float(e), None, ALU.is_equal)
            done(h)
            done(v.tensor_tensor_scan(cum[:].rearrange("p e t -> p (e t)"), zeros[:],
                                      one_hot[:].rearrange("p e t -> p (e t)"), 0.0, ALU.add, ALU.add))
            done(v.tensor_copy(ends[:, 1:E + 1], cum[:, :, NT - 1]))
            v.tensor_tensor(here[:], ends[:, 1:E + 1], ends[:, 0:E], ALU.subtract).then_inc(here_ok, 1)
            dve.wait_ge(consts, 4)
            v.tensor_copy(col[:], col_i[:])
            v.tensor_copy(col_bf[:], col_i[:, 0:col_bf.shape[1]])
            v.tensor_copy(row[:], row_i[:])
            dve.wait_ge(c_mm, 1)
            done(v.tensor_copy(counts[:], psC[:]))
            done(v.tensor_scalar(tiles_i[:], counts[:, 1], float(ST - 1), None, ALU.add))
            done(v.tensor_scalar(tiles_s[:], tiles_i[:], ST.bit_length() - 1, None, ALU.arith_shift_right))
            done(v.tensor_copy(tiles[:], tiles_s[:]))
            done(v.tensor_tensor_scan(tiles_cum[:], zeros[:, 0:E], tiles[:], 0.0, ALU.add, ALU.add))
            done(v.tensor_tensor(base[:], tiles_cum[:], tiles[:], ALU.subtract))
            done(v.tensor_scalar(base[:], base[:], float(ST), -1.0, ALU.mult, ALU.add))
            done(v.tensor_tensor(shift[:], base[:], counts[:, 0], ALU.add))
            done(v.tensor_tensor(shift[:], shift[:], ends[:, 0:E], ALU.subtract))
            done(v.tensor_tensor(cum[:], cum[:], shift[:].unsqueeze(2).to_broadcast([P, E, NT]), ALU.add))
            done(v.tensor_tensor(cum[:], cum[:], one_hot[:], ALU.mult))
            done(v.tensor_reduce(pos[:], cum[:].rearrange("p e t -> p t e"), AX.X, ALU.add))
            done(v.tensor_copy(pos_i[:], pos[:]))
            v.tensor_copy(keep.position[:], pos_i[:])
            v.tensor_scalar(lo_i[:], pos_i[:], P - 1, None, ALU.bitwise_and)
            done(v.tensor_scalar(hi_i[:], pos_i[:], P.bit_length() - 1, None, ALU.arith_shift_right))
            v.tensor_copy(lo[:], lo_i[:])
            done(v.tensor_copy(hi[:], hi_i[:]))

            def spread(i, last):
                for k in range(2):
                    t = 2 * i + k
                    wait(dve, s_mm, t - 1)
                    v.tensor_scalar(lo_hot[:, k], col_bf[:, 0:P], lo[:, bass.ds(t, 1)], None, ALU.is_equal)
                    v.tensor_scalar(hi_hot[:, k, 0], col_bf[:, 0:NC], hi[:, bass.ds(t, 1)], row[:, 0:1],
                                    ALU.is_equal, ALU.mult)
                    v.tensor_scalar(hi_hot[:, k, 1], col_bf[:, 0:NC], hi[:, bass.ds(t, 1)], col[:, bass.ds(t, 1)],
                                    ALU.is_equal, ALU.mult).then_inc(loop_ok, 1)
            each_pair(dve, NT // 2, spread)

            done(v.tensor_tensor(past[:], tiles_cum[0:1].unsqueeze(1).to_broadcast([1, ET, E]),
                                 col[0:1, 0:ET].unsqueeze(2).to_broadcast([1, ET, E]), ALU.is_le))
            done(v.tensor_reduce(tile_f[:], past[:], AX.X, ALU.add))
            done(v.tensor_scalar(tile_f[:], tile_f[:], float(E - 1), None, ALU.min))
            v.tensor_copy(keep.tile_expert[:], tile_f[:])
            dve.wait_ge(s_mm, NT)
            done(v.tensor_scalar(slot_t[:], psS[:, 1], float(P), None, ALU.mult))
            done(v.tensor_tensor(slot_f[:], slot_t[:], psS[:, 0], ALU.add))
            v.tensor_copy(keep.slot_token[:], slot_f[:])

        @block.tensor
        def _(pe):
            pe.wait_ge(here_ok, 1)
            pe.wait_ge(consts, 4)
            nc.tensor.matmul(psC[:, 0], below[:], here[:], start=True, stop=True)
            nc.tensor.matmul(psC[:, 1], ones[:], here[:], start=True, stop=True).then_inc(c_mm, 1)

            def gather(i, last):
                for k in range(2):
                    t = 2 * i + k
                    wait(pe, loop_ok, t + 1)
                    first = is_first(t)
                    nc.tensor.matmul(psS[:].rearrange("p a n -> p (a n)"), lo_hot[:, k],
                                     hi_hot[:, k].rearrange("p a n -> p (a n)"), start=first,
                                     stop=(last and k == 1), skip_group_check=True).then_inc(s_mm, 1)
            each_pair(pe, NT // 2, gather)


def expert_stage(nc, xs, rgw, ruw, rdw, d_t, keep, D, F, E, ET):
    C, H, IT = D // P, ST // P, F // P
    Q = IT // 2
    with ExitStack() as st:
        def sb(name, shape, dt=F32):
            return st.enter_context(nc.sbuf_tensor("e_" + name, shape, dt))

        def ps(name, shape):
            return st.enter_context(nc.psum_tensor("e_" + name, shape, F32))

        def sem(name):
            return st.enter_context(nc.semaphore("e_" + name))

        raw = [sb(f"raw{k}", [P, 3, C * F]) for k in range(2)]
        whi = [sb(f"whi{k}", [P, 3, C * F], F32R) for k in range(2)]
        wlo = [sb(f"wlo{k}", [P, 3, C * F], F32R) for k in range(2)]
        slot = sb("slot", [P, 2, H], I32)
        xg = sb("xg", [P, 2, H, D])
        x_hi = sb("x_hi", [P, 2, C, ST], F32R)
        x_lo = sb("x_lo", [P, 2, C, ST], F32R)
        silu = sb("silu", [P, 2, 2 * ST])
        h32 = sb("h32", [P, 2, 2 * ST])
        h_hi = [sb(f"h_hi{k}", [P, Q, 2 * ST], F32R) for k in range(2)]
        h_lo = [sb(f"h_lo{k}", [P, Q, 2 * ST], F32R) for k in range(2)]
        dout = sb("dout", [P, 2, H, D])
        psT = ps("psT", [P, C, ST])
        psG = ps("psG", [P, 2, 2, ST])
        psU = ps("psU", [P, 2, 2, ST])
        psD = ps("psD", [P, H, D])
        w_in = [sem(f"w_in{k}") for k in range(2)]
        x_in = [sem(f"x_in{k}") for k in range(2)]
        d_out = [sem(f"d_out{k}") for k in range(2)]
        passed = sem("passed")
        slot_ok, t_mm, xh_ok, xl_ok, whi_ok, wlo_ok = (sem(n) for n in ("slot_ok", "t_mm", "xh_ok", "xl_ok", "whi_ok", "wlo_ok"))
        g_mm, u_mm, silu_ok, h_ok, hhi_ok, hlo_ok, d_mm, do_ok = (
            sem(n) for n in ("g_mm", "u_mm", "silu_ok", "h_ok", "hhi_ok", "hlo_ok", "d_mm", "do_ok"))
        block = st.enter_context(nc.Block())

        def part(w, k, n):
            v = w[k][:, n]
            return v.rearrange("p (c f) -> p c f", c=C) if n < 2 else v.rearrange("p (i d) -> p i d", i=IT)

        @block.sync
        def _(sp):
            def load(t, k):
                wait(sp, whi_ok, 3 * (t - 1))
                wait(sp, wlo_ok, 3 * (t - 1))
                e = sp.value_load(keep.tile_expert[0:1, bass.ds(t, 1)], min_val=0, max_val=E - 1)
                sp.dma_start(part(raw, k, 0), rgw[e].rearrange("(c p) f -> p c f", p=P)).then_inc(w_in[k], 16)
                sp.dma_start(part(raw, k, 1), ruw[e].rearrange("(c p) f -> p c f", p=P)).then_inc(w_in[k], 16)
                sp.dma_start(part(raw, k, 2), rdw[e].rearrange("(i p) d -> p i d", p=P)).then_inc(w_in[k], 16)

            def store(t, k):
                wait(sp, do_ok, t + 1)
                sp.dma_start(d_t[t], dout[:, k]).then_inc(d_out[k], 16)

            load(0, 0)
            load(1, 1)

            def pair(i, last):
                for k in range(2):
                    t = 2 * i + k
                    if not last:
                        load(t + 2, k)
                    if not is_first(t):
                        store(t - 1, 1 - k)
            each_pair(sp, ET // 2, pair)
            store(ET - 1, 1)
            for k in range(2):
                sp.wait_ge(d_out[k], 16 * (ET // 2))

        @block.gpsimd
        def _(pool):
            g = nc.gpsimd

            def gather(t, k, i):
                wait_apart(pool, x_in[k], 16 * H * i, passed)
                g.tensor_copy(slot[:, k], keep.slot_token[:, bass.ds(t * H, H)]).then_inc(slot_ok, 1)
                wait(pool, t_mm, t - 1)
                wait_apart(pool, slot_ok, t + 1, passed)
                for h in range(H):
                    g.indirect_dma_start(out=xg[:, k, h], out_offset=None, in_=xs,
                                         in_offset=bass.IndirectOffsetOnAxis(slot[:, k, h:h + 1], 0)).then_inc(x_in[k], 16)

            def high(t, k, i):
                for n in range(3):
                    if n == 0:
                        wait(pool, u_mm, Q * (t - 1))
                        wait_apart(pool, w_in[k], 48 * (i + 1), passed)
                    if n == 2:
                        wait_apart(pool, d_mm, t - 1, passed)
                    g.tensor_copy(whi[k][:, n], raw[k][:, n]).then_inc(whi_ok, 1)

            gather(0, 0, 0)
            gather(1, 1, 0)
            high(0, 0, 0)

            def pair(i, last):
                for k in range(2):
                    t = 2 * i + k
                    if not last:
                        gather(t + 2, k, i + 1)
                    if not (last and k == 1):
                        high(t + 1, 1 - k, i + k)
            each_pair(pool, ET // 2, pair)

        @block.vector
        def _(dve):
            v = nc.vector

            def low(t, k, n):
                wait(dve, whi_ok, 3 * t + n + 1)
                v.tensor_tensor(wlo[k][:, n], raw[k][:, n], whi[k][:, n].bitcast(F32), ALU.subtract).then_inc(wlo_ok, 1)

            def x_low(t, k):
                wait(dve, xh_ok, t + 1)
                v.tensor_tensor(x_lo[:, k], psT[:], x_hi[:, k].bitcast(F32), ALU.subtract).then_inc(xl_ok, 1)

            def mul(t, q):
                wait(dve, u_mm, Q * t + q + 1)
                wait(dve, silu_ok, Q * t + q + 1)
                wait(dve, hlo_ok, Q * (t - 1) + q + 1)
                v.tensor_tensor(h32[:, q], silu[:, q], psU[:, q].rearrange("p a n -> p (a n)"), ALU.mult).then_inc(h_ok, 1)

            def h_low(t, k, q):
                wait(dve, hhi_ok, Q * t + q + 1)
                v.tensor_tensor(h_lo[k][:, q], h32[:, q], h_hi[k][:, q].bitcast(F32), ALU.subtract).then_inc(hlo_ok, 1)

            for n in range(3):
                low(0, 0, n)
            x_low(0, 0)

            def pair(i, last):
                for k in range(2):
                    t = 2 * i + k
                    more = not (last and k == 1)
                    if more:
                        low(t + 1, 1 - k, 0)
                    mul(t, 0)
                    if more:
                        low(t + 1, 1 - k, 1)
                    h_low(t, k, 0)
                    mul(t, 1)
                    if more:
                        x_low(t + 1, 1 - k)
                    h_low(t, k, 1)
                    if more:
                        low(t + 1, 1 - k, 2)
            each_pair(dve, ET // 2, pair)

        @block.scalar
        def _(act):
            s = nc.scalar

            def x_high(t, k):
                wait(act, t_mm, t + 1)
                s.copy(x_hi[:, k], psT[:]).then_inc(xh_ok, 1)

            def silu_of(t, q):
                wait(act, g_mm, Q * t + q + 1)
                wait(act, h_ok, Q * (t - 1) + q + 1)
                s.activation(silu[:, q], psG[:, q].rearrange("p a n -> p (a n)"), ACT.Silu).then_inc(silu_ok, 1)

            def h_high(t, k, q):
                wait(act, h_ok, Q * t + q + 1)
                s.copy(h_hi[k][:, q], h32[:, q]).then_inc(hhi_ok, 1)

            def d_copy(t, k, i):
                wait(act, d_mm, t + 1)
                wait(act, d_out[k], 16 * i)
                s.copy(dout[:, k], psD[:]).then_inc(do_ok, 1)

            x_high(0, 0)

            def pair(i, last):
                for k in range(2):
                    t = 2 * i + k
                    silu_of(t, 0)
                    h_high(t, k, 0)
                    silu_of(t, 1)
                    h_high(t, k, 1)
                    if not (last and k == 1):
                        x_high(t + 1, 1 - k)
                    if not is_first(t):
                        d_copy(t - 1, 1 - k, i - 1 + k)
            each_pair(act, ET // 2, pair)
            d_copy(ET - 1, 1, ET // 2 - 1)

        @block.tensor
        def _(pe):
            def transposes(t, k, i):
                wait(pe, x_in[k], 16 * H * (i + 1))
                wait(pe, xl_ok, t)
                for c in range(C):
                    for h in range(H):
                        mm = nc.tensor.transpose(psT[:, c, h * P:(h + 1) * P], xg[:, k, h, c * P:(c + 1) * P], keep.ident[:])
                mm.then_inc(t_mm, 1)

            def up(t, k):
                wait(pe, xl_ok, t + 1)
                for q in range(Q):
                    for n, (psum, freed, out) in enumerate(((psG, silu_ok, g_mm), (psU, h_ok, u_mm))):
                        wait(pe, wlo_ok, 3 * t + n + 1)
                        wait(pe, freed, Q * (t - 1) + q + 1)
                        for a in range(2):
                            cols = slice((2 * q + a) * P, (2 * q + a + 1) * P)
                            for c in range(C):
                                mm = split_matmuls(nc, psum[:, q, a], part(whi, k, n)[:, c, cols], part(wlo, k, n)[:, c, cols],
                                                   x_hi[:, k, c], x_lo[:, k, c], c == 0, c == C - 1)
                        mm.then_inc(out, 1)

            def down(t, k):
                wait(pe, wlo_ok, 3 * t + 3)
                wait(pe, do_ok, t)
                for it in range(IT):
                    wait(pe, hlo_ok, Q * t + it // 2 + 1)
                    for h in range(H):
                        cols = slice((it % 2) * ST + h * P, (it % 2) * ST + (h + 1) * P)
                        mm = split_matmuls(nc, psD[:, h], h_hi[k][:, it // 2, cols], h_lo[k][:, it // 2, cols],
                                           part(whi, k, 2)[:, it], part(wlo, k, 2)[:, it],
                                           it == 0 and h == 0, it == IT - 1)
                mm.then_inc(d_mm, 1)

            transposes(0, 0, 0)

            def pair(i, last):
                for k in range(2):
                    t = 2 * i + k
                    up(t, k)
                    if not (last and k == 1):
                        transposes(t + 1, 1 - k, i + k)
                    if not is_first(t):
                        down(t - 1, 1 - k)
            each_pair(pe, ET // 2, pair)
            down(ET - 1, 1)


def attention_stage(nc, x_g, sh_g, d_rows, xth_g, xtl_g, out_g, keep, D, B, N):
    C, NB, GB = D // P, N // P, N // GT
    J = GT // P
    QU = C * GB
    VU = NB // 2
    groups = [i // 4 + 1 for i in range(NB)]
    before = [sum(groups[:i]) for i in range(NB + 1)]
    TG = before[NB]
    assert TG % 4 == 0 and NB % 2 == 0
    with ExitStack() as st:
        def sb(name, shape, dt=F32):
            return st.enter_context(nc.sbuf_tensor("t_" + name, shape, dt))

        def ps(name, shape):
            return st.enter_context(nc.psum_tensor("t_" + name, shape, F32))

        def sem(name):
            return st.enter_context(nc.semaphore("t_" + name))

        x_hi = [sb(f"x_hi{k}", [P, C, N], F32R) for k in range(2)]
        x_lo = [sb(f"x_lo{k}", [P, C, N], F32R) for k in range(2)]
        q_hi = sb("q_hi", [P, C, N], F32R)
        q_lo = sb("q_lo", [P, C, N], F32R)
        v_hi = sb("v_hi", [P, NB, D], F32R)
        v_lo = sb("v_lo", [P, NB, D], F32R)
        prob = [sb(f"prob{k}", [P, N]) for k in range(2)]
        pT_hi = [sb(f"pT_hi{k}", [P, 4, P], F32R) for k in range(4)]
        pT_lo = [sb(f"pT_lo{k}", [P, 4, P], F32R) for k in range(4)]
        xr = sb("xr", [P, 2, J, D])
        shr = sb("shr", [P, 2, J, D])
        pos = sb("pos", [P, 2, 1], I32)
        routed = sb("routed", [P, 2, D])
        sum1 = sb("sum1", [P, 2, D])
        base = sb("base", [P, 2, D])
        negmax = sb("negmax", [P, 2])
        rowsum = sb("rowsum", [P, 2])
        rinv = sb("rinv", [P, 2])
        outb = sb("outb", [P, 2, D])
        psS = ps("psS", [P, 4, 512])
        psT = ps("psT", [P, 2, 4, P])
        psO = ps("psO", [P, 2, 512])
        x_in = [sem(f"x_in{k}") for k in range(2)]
        r_in = [sem(f"r_in{k}") for k in range(2)]
        d_in = [sem(f"d_in{k}") for k in range(2)]
        o_out = [sem(f"o_out{k}") for k in range(2)]
        q_mm, qh_ok, ql_ok, v_mm, vh_ok, vl_ok = (sem(n) for n in ("q_mm", "qh_ok", "ql_ok", "v_mm", "vh_ok", "vl_ok"))
        s_mm, max_ok, exp_ok, t_mm, ph_ok, pl_ok, pv_mm, o_ok, rinv_ok = (
            sem(n) for n in ("s_mm", "max_ok", "exp_ok", "t_mm", "ph_ok", "pl_ok", "pv_mm", "o_ok", "rinv_ok"))
        passed = sem("passed")
        pos_ok, sum_ok, base_ok = (sem(n) for n in ("pos_ok", "sum_ok", "base_ok"))
        block = st.enter_context(nc.Block())

        def width(i):
            n = (i + 1) * P
            return [min(512, -(-(n - c) // 256) * 256) for c in range(0, n, 512)]

        @block.sync
        def _(sp):
            def load_xt(b, k):
                wait(sp, s_mm, NB * (b - 1))
                for g in range(GB):
                    cols = slice(g * GT, (g + 1) * GT)
                    sp.dma_start(x_hi[k][:, :, cols].bitcast(F32), xth_g[b * GB + g]).then_inc(x_in[k], 16)
                    sp.dma_start(x_lo[k][:, :, cols].bitcast(F32), xtl_g[b * GB + g]).then_inc(x_in[k], 16)

            def load_rows(n, k):
                wait(sp, base_ok, J * (n - 1))
                sp.dma_start(xr[:, k], x_g[n]).then_inc(r_in[k], 16)
                sp.dma_start(shr[:, k], sh_g[n]).then_inc(r_in[k], 16)

            load_xt(0, 0)
            load_rows(0, 0)
            load_rows(1, 1)
            load_xt(1, 1)

            def pair(i, last):
                for k in range(2):
                    b = 2 * i + k
                    for g in range(GB):
                        for j in range(J):
                            r = b * NB + g * J + j
                            wait(sp, o_ok, r + 1)
                            sp.dma_start(out_g[b * GB + g][:, j], outb[:, j % 2]).then_inc(o_out[j % 2], 16)
                        if not (last and k == 1 and g >= GB - 2):
                            load_rows(b * GB + g + 2, g % 2)
                    if not last:
                        load_xt(b + 2, k)
            each_pair(sp, B // 2, pair)
            for k in range(2):
                sp.wait_ge(o_out[k], 16 * (B * NB // 2))

        @block.gpsimd
        def _(pool):
            g = nc.gpsimd

            def gather(r, k, n):
                wait(pool, sum_ok, r - 1)
                wait_apart(pool, d_in[k], 16 * n, passed)
                g.tensor_copy(pos[:, k], keep.position[:, bass.ds(r, 1)]).then_inc(pos_ok, 1)
                wait_apart(pool, pos_ok, r + 1, passed)
                g.indirect_dma_start(out=routed[:, k], out_offset=None, in_=d_rows,
                                     in_offset=bass.IndirectOffsetOnAxis(pos[:, k, 0:1], 0)).then_inc(d_in[k], 16)

            gather(0, 0, 0)
            gather(1, 1, 0)

            def pair(i, last):
                for t in range(2 * NB):
                    r = i * 2 * NB + t
                    k, kg, j = t % 2, (t // J) % 2, t % J
                    if j == 0:
                        wait(pool, r_in[kg], 32 * (i * GB + t // (2 * J) + 1))
                    wait(pool, d_in[k], 16 * (i * NB + t // 2 + 1))
                    wait(pool, o_ok, r - 1)
                    g.tensor_tensor(sum1[:, k], routed[:, k], shr[:, kg, j], ALU.add).then_inc(sum_ok, 1)
                    wait(pool, sum_ok, r + 1)
                    g.tensor_tensor(base[:, k], sum1[:, k], xr[:, kg, j], ALU.add).then_inc(base_ok, 1)
                    if not (last and t >= 2 * NB - 2):
                        gather(r + 2, k, i * NB + t // 2 + 1)
            each_pair(pool, B // 2, pair)

        @block.vector
        def _(dve):
            v = nc.vector

            def q_low(b, u):
                wait(dve, qh_ok, QU * b + u + 1)
                c, n = u % C, u // C
                v.tensor_tensor(q_lo[:, c, n * 512:(n + 1) * 512], psS[:, u % 4],
                                q_hi[:, c, n * 512:(n + 1) * 512].bitcast(F32), ALU.subtract).then_inc(ql_ok, 1)

            def v_low(b, u):
                wait(dve, vh_ok, VU * b + u + 1)
                v.tensor_tensor(v_lo[:, 2 * u:2 * u + 2].rearrange("p a d -> p (a d)"), psS[:, u % 4],
                                v_hi[:, 2 * u:2 * u + 2].rearrange("p a d -> p (a d)").bitcast(F32),
                                ALU.subtract).then_inc(vl_ok, 1)

            def row_max(b, i):
                r = b * NB + i
                wait(dve, s_mm, r + 1)
                wait(dve, exp_ok, r - 1)
                v.tensor_reduce(negmax[:, i % 2:i % 2 + 1], psS[:].rearrange("p a n -> p (a n)")[:, 0:(i + 1) * P],
                                AX.X, ALU.max, negate=True).then_inc(max_ok, 1)

            def p_low(b, i, q):
                n = b * TG + before[i] + q
                s = (before[i] + q) % 4
                m = min(4, i + 1 - 4 * q)
                wait(dve, ph_ok, n + 1)
                v.tensor_tensor(pT_lo[s][:, 0:m], psT[:, s % 2, 0:m], pT_hi[s][:, 0:m].bitcast(F32),
                                ALU.subtract).then_inc(pl_ok, 1)

            def output(b, i, half):
                r = b * NB + i
                k = i % 2
                v.reciprocal(rinv[:, k:k + 1], rowsum[:, k:k + 1]).then_inc(rinv_ok, 1)
                wait(dve, rinv_ok, r + 1)
                wait(dve, pv_mm, b * TG + before[i + 1])
                wait(dve, base_ok, r + 1)
                wait(dve, o_out[k], 16 * half)
                v.scalar_tensor_tensor(out=outb[:, k], in0=psO[:, k, 0:D], scalar=rinv[:, k:k + 1], in1=base[:, k],
                                       op0=ALU.mult, op1=ALU.add).then_inc(o_ok, 1)

            for u in range(QU):
                q_low(0, u)

            def pair(p, last):
                for k in range(2):
                    b = 2 * p + k
                    for u in range(VU):
                        v_low(b, u)
                    row_max(b, 0)
                    for i in range(NB):
                        for q in range(min(2, groups[i])):
                            p_low(b, i, q)
                        if i + 1 < NB:
                            row_max(b, i + 1)
                        elif not (last and k == 1):
                            for u in range(QU // 2):
                                q_low(b + 1, u)
                        for q in range(2, groups[i]):
                            p_low(b, i, q)
                        if i + 1 == NB and not (last and k == 1):
                            for u in range(QU // 2, QU):
                                q_low(b + 1, u)
                        output(b, i, b * (NB // 2) + i // 2)
            each_pair(dve, B // 2, pair)

        @block.scalar
        def _(act):
            s = nc.scalar

            def q_high(b, u):
                c, n = u % C, u // C
                wait(act, q_mm, QU * b + u + 1)
                s.copy(q_hi[:, c, n * 512:(n + 1) * 512], psS[:, u % 4]).then_inc(qh_ok, 1)

            def v_high(b, u):
                wait(act, v_mm, VU * b + u + 1)
                s.copy(v_hi[:, 2 * u:2 * u + 2].rearrange("p a d -> p (a d)"), psS[:, u % 4]).then_inc(vh_ok, 1)

            def exp(b, i):
                r = b * NB + i
                wait(act, max_ok, r + 1)
                wait(act, o_ok, r - 1)
                s.activation(prob[i % 2][:, 0:(i + 1) * P], psS[:].rearrange("p a n -> p (a n)")[:, 0:(i + 1) * P],
                             ACT.Exp, bias=negmax[:, i % 2:i % 2 + 1], accum_out=rowsum[:, i % 2:i % 2 + 1]).then_inc(exp_ok, 1)

            def p_high(b, i, q):
                n = b * TG + before[i] + q
                t = (before[i] + q) % 4
                m = min(4, i + 1 - 4 * q)
                wait(act, t_mm, n + 1)
                wait(act, pv_mm, n - 3)
                s.copy(pT_hi[t][:, 0:m], psT[:, t % 2, 0:m]).then_inc(ph_ok, 1)

            for u in range(QU):
                q_high(0, u)

            def pair(p, last):
                for k in range(2):
                    b = 2 * p + k
                    for u in range(VU):
                        v_high(b, u)
                    exp(b, 0)
                    for i in range(NB):
                        for q in range(min(3, groups[i])):
                            p_high(b, i, q)
                            if q == 1 and i + 1 == NB and not (last and k == 1):
                                for u in range(QU // 2):
                                    q_high(b + 1, u)
                        for q in range(3, groups[i]):
                            p_high(b, i, q)
                        if i + 1 < NB:
                            exp(b, i + 1)
                        elif not (last and k == 1):
                            for u in range(QU // 2, QU):
                                q_high(b + 1, u)
            each_pair(act, B // 2, pair)

        @block.tensor
        def _(pe):
            def queries(b, k, u):
                c, n = u % C, u // C
                if u == 0:
                    wait(pe, x_in[k], 32 * GB * (b // 2 + 1) if isinstance(b, int) else 16 * GB * (b - k + 2))
                wait(pe, exp_ok, NB * b)
                if u >= 4:
                    wait(pe, ql_ok, QU * b + u - 3)
                for d in range(C):
                    mm = split_matmuls(nc, psS[:, u % 4], keep.a_hi[:, d, c * P:(c + 1) * P], keep.a_lo[:, d, c * P:(c + 1) * P],
                                       x_hi[k][:, d, n * 512:(n + 1) * 512], x_lo[k][:, d, n * 512:(n + 1) * 512],
                                       d == 0, d == C - 1)
                mm.then_inc(q_mm, 1)

            def values(b, k, u):
                if u < 4:
                    wait(pe, ql_ok, QU * (b + 1) - 3 + u)
                else:
                    wait(pe, vl_ok, VU * b + u - 3)
                for a in range(2):
                    cols = slice((2 * u + a) * P, (2 * u + a + 1) * P)
                    for d in range(C):
                        mm = split_matmuls(nc, psS[:, u % 4, a * D:(a + 1) * D], x_hi[k][:, d, cols], x_lo[k][:, d, cols],
                                           keep.v_hi[:, d], keep.v_lo[:, d], d == 0, d == C - 1)
                mm.then_inc(v_mm, 1)

            def scores(b, k, i):
                if i == 0:
                    wait(pe, vl_ok, VU * (b + 1))
                wait(pe, exp_ok, b * NB + i)
                rows = slice(i * P, (i + 1) * P)
                for n, w in enumerate(width(i)):
                    diagonal = n == i // 4
                    for d in range(C):
                        split_matmuls(nc, psS[:, n, 0:w], q_hi[:, d, rows], q_lo[:, d, rows],
                                      x_hi[k][:, d, n * 512:n * 512 + w], x_lo[k][:, d, n * 512:n * 512 + w],
                                      d == 0, d == C - 1 and not diagonal)
                mm = nc.tensor.matmul(psS[:, i // 4, (i % 4) * P:(i % 4 + 1) * P], keep.ident_bf[:], keep.mask_bf[:],
                                      start=False, stop=True, skip_group_check=True)
                mm.then_inc(s_mm, 1)

            def transposes(b, i, q):
                n = b * TG + before[i] + q
                s = (before[i] + q) % 2
                if q == 0:
                    wait(pe, exp_ok, b * NB + i + 1)
                wait(pe, pl_ok, n - 1)
                for m in range(4 * q, min(4 * q + 4, i + 1)):
                    mm = nc.tensor.transpose(psT[:, s, m % 4], prob[i % 2][:, m * P:(m + 1) * P], keep.ident[:])
                mm.then_inc(t_mm, 1)

            def weigh(b, i, q):
                n = b * TG + before[i] + q
                s = (before[i] + q) % 4
                wait(pe, pl_ok, n + 1)
                if q == 0:
                    wait(pe, o_ok, b * NB + i - 1)
                for m in range(4 * q, min(4 * q + 4, i + 1)):
                    mm = split_matmuls(nc, psO[:, i % 2, 0:D], pT_hi[s][:, m % 4], pT_lo[s][:, m % 4],
                                       v_hi[:, m], v_lo[:, m], m == 0, m == i)
                mm.then_inc(pv_mm, 1)

            for u in range(QU):
                queries(0, 0, u)

            def pair(p, last):
                for k in range(2):
                    b = 2 * p + k
                    for u in range(VU):
                        values(b, k, u)
                    scores(b, k, 0)
                    for i in range(NB):
                        for q in range(min(2, groups[i])):
                            transposes(b, i, q)
                        more = not (last and k == 1)
                        if i + 1 < NB:
                            scores(b, k, i + 1)
                        elif more:
                            for u in range(QU // 2):
                                queries(b + 1, 1 - k, u)
                        for q in range(groups[i]):
                            weigh(b, i, q)
                            if q + 2 < groups[i]:
                                transposes(b, i, q + 2)
                        if i + 1 == NB and more:
                            for u in range(QU // 2, QU):
                                queries(b + 1, 1 - k, u)
            each_pair(pe, B // 2, pair)


class Keep:

    def __init__(self, nc, ctx, D, NT, SC, ET):
        def sb(name, shape, dt):
            return ctx.enter_context(nc.sbuf_tensor("keep_" + name, shape, dt))

        C = D // P
        self.ident = sb("ident", [P, P], F32)
        self.ident_bf = sb("ident_bf", [P, P], BF16)
        self.mask_bf = sb("mask_bf", [P, P], BF16)
        self.a_hi = sb("a_hi", [P, C, D], F32R)
        self.a_lo = sb("a_lo", [P, C, D], F32R)
        self.v_hi = sb("v_hi", [P, C, D], F32R)
        self.v_lo = sb("v_lo", [P, C, D], F32R)
        self.neghalf = sb("neghalf", [P, GT // P], F32)
        self.euler = sb("euler", [P, GT // P], F32)
        self.expert = sb("expert", [P, NT], F32)
        self.position = sb("position", [P, NT], I32)
        self.slot_token = sb("slot_token", [P, SC], I32)
        self.tile_expert = sb("tile_expert", [1, ET], I32)


def build(nc, x, W_qkv, gate_w, sgw, suw, sdw, rgw, ruw, rdw, out):
    B, N, D = x.shape
    E, _, F = rgw.shape
    T = B * N
    NT, NG = T // P, T // GT
    ET = T // ST + E
    C = D // P
    x_g = x.rearrange("b n d -> (b n) d").rearrange("(g j p) d -> g p j d", p=P, j=GT // P)
    out_g = out.rearrange("b n d -> (b n) d").rearrange("(g j p) d -> g p j d", p=P, j=GT // P)
    xs = nc.dram_tensor("xs_rows", [T, D], F32).ap()
    sh = nc.dram_tensor("shared_rows", [T, D], F32).ap()
    dr = nc.dram_tensor("routed_rows", [ET * ST, D], F32).ap()
    xth = nc.dram_tensor("xT_high", [NG, P, C, GT], F32).ap()
    xtl = nc.dram_tensor("xT_low", [NG, P, C, GT], F32).ap()
    xs_g = xs.rearrange("(g j p) d -> g p j d", p=P, j=GT // P)
    sh_g = sh.rearrange("(g j p) d -> g p j d", p=P, j=GT // P)
    d_t = dr.rearrange("(t h p) d -> t p h d", p=P, h=ST // P)
    with ExitStack() as ctx:
        keep = Keep(nc, ctx, D, NT, ET * ST // P, ET)
        setup_stage(nc, ctx, W_qkv, keep, D)
        token_stage(nc, x_g, gate_w, sgw, suw, sdw, xs_g, xth, xtl, sh_g, keep, D, F, E, NG)
        routing_stage(nc, keep, E, NT, ET)
        expert_stage(nc, xs, rgw, ruw, rdw, d_t, keep, D, F, E, ET)
        attention_stage(nc, x_g, sh_g, dr, xth, xtl, out_g, keep, D, B, N)


_INS = ["L0_attn_x", "L0_attn_W_qkv", "L0_ffn_gate_w", "L0_ffn_shared_gate_w", "L0_ffn_shared_up_w",
        "L0_ffn_shared_down_w", "L0_ffn_routed_gate_w", "L0_ffn_routed_up_w", "L0_ffn_routed_down_w"]


def kernel(**inputs):
    import numpy as np
    from concourse import bacc
    from concourse.bass_utils import run_bass_kernel_spmd

    nc = bacc.Bacc("TRN2", target_bir_lowering=False, num_devices=1)
    arrays = {f"in_{n}": np.ascontiguousarray(inputs[n]) for n in _INS}
    args = [nc.dram_tensor(n, a.shape, mybir.dt.from_np(a.dtype), kind="ExternalInput").ap() for n, a in arrays.items()]
    out = nc.dram_tensor("out", inputs["L0_attn_x"].shape, F32, kind="ExternalOutput").ap()
    build(nc, *args, out)
    return run_bass_kernel_spmd(nc, [arrays], core_ids=[0]).results[0]["out"]
```

```python
from contextlib import ExitStack

import concourse.bass as bass
from concourse import mybir

F32 = mybir.dt.float32
F32R = mybir.dt.float32r
BF16 = mybir.dt.bfloat16
I32 = mybir.dt.int32
U32 = mybir.dt.uint32
ALU = mybir.AluOpType
ACT = mybir.ActivationFunctionType
AX = mybir.AxisListType

P = 128
EPS = 1e-5
EULER = 2.718281828459045
MASKED = -1e30
GT = 512
ST = 256


def wait(eng, sem, value):
    if isinstance(value, int) and value <= 0:
        return
    eng.wait_ge(sem, value)


def is_first(g):
    return isinstance(g, int) and g == 0


def wait_apart(eng, sem, value, passed):
    if isinstance(value, int) and value <= 0:
        return
    eng.wait_ge(sem, value)
    eng.sem_inc(passed, 1)


def each_pair(eng, n, body):
    for i in range(min(2, n - 1)):
        body(i, False)
    if n > 3:
        with eng.Fori(2, n - 1) as i:
            body(i, False)
    body(n - 1, True)


def split_matmuls(nc, out, hi, lo, rhi, rlo, first, last):
    nc.tensor.matmul(out, hi, rhi, start=first, stop=False, skip_group_check=True)
    nc.tensor.matmul(out, lo, rhi, start=False, stop=False, skip_group_check=True)
    return nc.tensor.matmul(out, hi, rlo, start=False, stop=last, skip_group_check=True)


def token_stage(nc, x_g, gate_w, sgw, suw, sdw, xs_g, xth_g, xtl_g, sh_g, keep, ranks, D, F, E, NG):
    C, J, IT = D // P, GT // P, F // P
    with ExitStack() as st:
        def sb(name, shape, dt=F32):
            return st.enter_context(nc.sbuf_tensor("a_" + name, shape, dt))

        def ps(name, shape):
            return st.enter_context(nc.psum_tensor("a_" + name, shape, F32))

        def sem(name):
            return st.enter_context(nc.semaphore("a_" + name))

        wraw = sb("wraw", [P, 3, IT * D])
        raw = [wraw[:, 0].rearrange("p (c f) -> p c f", c=C), wraw[:, 1].rearrange("p (c f) -> p c f", c=C),
               wraw[:, 2].rearrange("p (i d) -> p i d", i=IT)]
        w_hi = [sb("gw_hi", [P, C, F], F32R), sb("uw_hi", [P, C, F], F32R), sb("dw_hi", [P, IT, D], F32R)]
        w_lo = [sb("gw_lo", [P, C, F], F32R), sb("uw_lo", [P, C, F], F32R), sb("dw_lo", [P, IT, D], F32R)]
        maskf = sb("maskf", [P, P])
        expert_i = sb("expert_i", [P, E], I32)
        expert_f = sb("expert_f", [P, E])
        seen = sb("seen", [P, J + 1, E])
        mine = sb("mine", [P, J, E])
        gate = sb("gate", [P, C, E])
        gate_hl = sb("gate_hl", [P, C, 2, E], F32R)
        xt = sb("xt", [P, 2, J, D])
        stats = sb("stats", [P, 2, J, 6])
        mv = sb("mv", [P, 2, J, 2])
        ve = sb("ve", [P, 2, J])
        rstd = sb("rstd", [P, 2, J])
        xn = sb("xn", [P, 2, J, D])
        xT_hi = [sb(f"xT_hi{k}", [P, C, GT], F32R) for k in range(2)]
        xT_lo = [sb(f"xT_lo{k}", [P, C, GT], F32R) for k in range(2)]
        silu = sb("silu", [P, 2, GT])
        h32 = sb("h32", [P, IT, GT])
        h_hi = [sb(f"h_hi{k}", [P, IT, GT], F32R) for k in range(2)]
        h_lo = [sb(f"h_lo{k}", [P, IT, GT], F32R) for k in range(2)]
        sh = sb("sh", [P, 2, J, D])
        lg2 = sb("lg2", [P, J, 2, E])
        lg = sb("lg", [P, J, E])
        top = sb("top", [P, J, 8])
        topi = sb("topi", [P, J, 8], U32)
        negtop = sb("negtop", [P, J])
        eneg = sb("eneg", [P, J])
        score = sb("score", [P, 2, J])
        xs = sb("xs", [P, 2, J, D])
        psT = ps("psT", [P, 2, 512])
        psG = ps("psG", [P, 2, 512])
        psU = ps("psU", [P, 2, 512])
        psD = ps("psD", [P, J, D])
        psL = psT[:, 0, 0:J * 2 * E].rearrange("p (j n) -> p j n", j=J)

        gate_in, w_hi_ok, w_ok, gate_ok = (sem(n) for n in ("gate_in", "w_hi_ok", "w_ok", "gate_ok"))
        w_in = [sem(f"w_in{n}") for n in range(3)]
        x_in = [sem(f"x_in{k}") for k in range(2)]
        xs_out = [sem(f"xs_out{k}") for k in range(2)]
        xt_out = [sem(f"xt_out{k}") for k in range(2)]
        sh_out = [sem(f"sh_out{k}") for k in range(2)]
        var_ok, rstd_ok, xn_ok, t_mm, xh_ok, xl_ok = (sem(n) for n in ("var_ok", "rstd_ok", "xn_ok", "t_mm", "xh_ok", "xl_ok"))
        g_mm, u_mm, silu_ok, h_ok, hhi_ok, hlo_ok, d_mm, sh_ok = (
            sem(n) for n in ("g_mm", "u_mm", "silu_ok", "h_ok", "hhi_ok", "hlo_ok", "d_mm", "sh_ok"))
        lg_mm, lg_ok, ntop_ok, eneg_ok, xs_ok, rt_step = (
            sem(n) for n in ("lg_mm", "lg_ok", "ntop_ok", "eneg_ok", "xs_ok", "rt_step"))
        rk_step, sg_step = sem("rk_step"), sem("sg_step")
        ln_step, passed, zeroed, ident_ok, iota_ok = (sem(n) for n in ("ln_step", "passed", "zeroed", "ident_ok", "iota_ok"))
        block = st.enter_context(nc.Block())

        @block.sync
        def _(sp):
            sp.dma_start(xt[:, 0], x_g[0]).then_inc(x_in[0], 16)
            sp.dma_start(gate[:], gate_w.rearrange("(c p) e -> p c e", p=P)).then_inc(gate_in, 16)
            sp.dma_start(raw[0], sgw.rearrange("(c p) f -> p c f", p=P)).then_inc(w_in[0], 16)
            sp.dma_start(raw[1], suw.rearrange("(c p) f -> p c f", p=P)).then_inc(w_in[1], 16)
            sp.dma_start(raw[2], sdw.rearrange("(i p) d -> p i d", p=P)).then_inc(w_in[2], 16)
            sp.dma_start(xt[:, 1], x_g[1]).then_inc(x_in[1], 16)

            def store_xt(g, k):
                wait(sp, xh_ok, C * (g + 1))
                sp.dma_start(xth_g[g], xT_hi[k][:].bitcast(F32)).then_inc(xt_out[k], 16)
                wait(sp, xl_ok, C * (g + 1))
                sp.dma_start(xtl_g[g], xT_lo[k][:].bitcast(F32)).then_inc(xt_out[k], 16)

            def store_xs(g, k):
                wait(sp, xs_ok, g + 1)
                sp.dma_start(xs_g[g], xs[:, k]).then_inc(xs_out[k], 16)

            def store_sh(g, k):
                wait(sp, sh_ok, g + 1)
                sp.dma_start(sh_g[g], sh[:, k]).then_inc(sh_out[k], 16)

            store_xt(0, 0)

            def pair(i, last):
                for k in range(2):
                    g = 2 * i + k
                    if not last:
                        wait(sp, xn_ok, g + 1)
                        sp.dma_start(xt[:, k], x_g[g + 2]).then_inc(x_in[k], 16)
                    store_xs(g, k)
                    if not (last and k == 1):
                        store_xt(g + 1, 1 - k)
                    if not is_first(g):
                        store_sh(g - 1, 1 - k)
            each_pair(sp, NG // 2, pair)
            store_sh(NG - 1, 1)
            for k in range(2):
                sp.wait_ge(xt_out[k], 32 * (NG // 2))
                sp.wait_ge(xs_out[k], 16 * (NG // 2))
                sp.wait_ge(sh_out[k], 16 * (NG // 2))

        @block.gpsimd
        def _(pool):
            def rstd_of(g, k):
                wait(pool, var_ok, g + 1)
                nc.gpsimd.tensor_tensor(rstd[:, k], ve[:, k], keep.neghalf[:], ALU.pow).then_inc(rstd_ok, 1)

            def eneg_of(g):
                wait(pool, ntop_ok, g + 1)
                nc.gpsimd.tensor_tensor(eneg[:], keep.euler[:], negtop[:], ALU.pow).then_inc(eneg_ok, 1)

            g = nc.gpsimd
            g.memset(keep.neghalf[:], -0.5).then_inc(zeroed, 1)
            g.memset(keep.euler[:], EULER).then_inc(zeroed, 1)
            g.memset(keep.ident[:], 0.0).then_inc(zeroed, 1)
            g.memset(maskf[:], 0.0).then_inc(zeroed, 1)
            pool.wait_ge(zeroed, 4)
            g.affine_select(out=keep.ident[:], in_=keep.ident[:], compare_op=ALU.not_equal, fill=1.0,
                            base=0, pattern=[[-1, P]], channel_multiplier=1).then_inc(ident_ok, 1)
            g.iota(expert_i[:], pattern=[[1, E]], base=0, channel_multiplier=0).then_inc(iota_ok, 1)
            rstd_of(0, 0)
            g.affine_select(out=maskf[:], in_=maskf[:], compare_op=ALU.is_ge, fill=MASKED,
                            base=0, pattern=[[-1, P]], channel_multiplier=1).then_inc(ident_ok, 1)
            rstd_of(1, 1)

            def pair(i, last):
                for k in range(2):
                    g = 2 * i + k
                    eneg_of(g)
                    if not last:
                        rstd_of(g + 2, k)
            each_pair(pool, NG // 2, pair)

        @block.vector
        def _(dve):
            v = nc.vector
            v.memset(seen[:, 0], 0.0).then_inc(rt_step, 1)
            dve.wait_ge(gate_in, 16)
            v.tensor_copy(gate_hl[:, :, 0], gate[:]).then_inc(gate_ok, 1)
            dve.wait_ge(gate_ok, 1)
            v.tensor_tensor(gate_hl[:, :, 1], gate[:], gate_hl[:, :, 0].bitcast(F32), ALU.subtract).then_inc(gate_ok, 1)

            def stats_of(g, k, i):
                wait(dve, x_in[k], 16 * (i + 1))
                for j in range(J):
                    s = v.bn_stats(stats[:, k, j], xt[:, k, j])
                s.then_inc(ln_step, 1)
                wait_apart(dve, ln_step, 2 * g + 1, passed)
                for j in range(J):
                    s = v.bn_aggr(mv[:, k, j], stats[:, k, j])
                s.then_inc(ln_step, 1)
                wait(dve, ln_step, 2 * g + 2)
                v.tensor_scalar(ve[:, k], mv[:, k, :, 1], EPS, None, ALU.add).then_inc(var_ok, 1)

            def norm(g, k):
                wait(dve, rstd_ok, g + 1)
                for j in range(J):
                    s = v.tensor_scalar(xn[:, k, j], xt[:, k, j], mv[:, k, j, 0:1], rstd[:, k, j:j + 1],
                                        ALU.subtract, ALU.mult)
                s.then_inc(xn_ok, 1)

            def xT_low(g, k, i):
                wait(dve, xt_out[k], 32 * i)
                for c in range(C):
                    wait(dve, xh_ok, C * g + c + 1)
                    v.tensor_tensor(xT_lo[k][:, c], psT[:, c], xT_hi[k][:, c].bitcast(F32), ALU.subtract).then_inc(xl_ok, 1)

            RS = J + 5

            def route(g):
                n = RS * g + 1
                wait(dve, lg_ok, g + 1)
                v.tensor_tensor(lg[:], lg2[:, :, 0], lg2[:, :, 1], ALU.add).then_inc(rt_step, 1)
                wait_apart(dve, rt_step, n + 1, passed)
                for j in range(J):
                    s = v.max(top[:, j], lg[:, j])
                s.then_inc(rt_step, 1)
                wait(dve, rt_step, n + 2)
                v.tensor_scalar(negtop[:], top[:, :, 0], -1.0, None, ALU.mult).then_inc(ntop_ok, 1)
                for j in range(J):
                    s = v.max_index(topi[:, j], top[:, j], lg[:, j])
                s.then_inc(rt_step, 1)

            def rank(g):
                n = RS * g + 4
                wait(dve, rt_step, n)
                for j in range(J):
                    s = v.tensor_scalar(ranks.one_hot[:, bass.ds(g * J + j, 1)].rearrange("p a e -> p (a e)"),
                                        expert_f[:], topi[:, j, 0:1], None, ALU.is_equal)
                s.then_inc(rt_step, 1)
                for j in range(J):
                    wait(dve, rt_step, n + 1 + j)
                    v.tensor_tensor(seen[:, j + 1], seen[:, j],
                                    ranks.one_hot[:, bass.ds(g * J + j, 1)].rearrange("p a e -> p (a e)"),
                                    ALU.add).then_inc(rt_step, 1)

            def rank_sum(g):
                n = RS * g + J + 5
                wait(dve, rt_step, n)
                v.tensor_tensor(mine[:], seen[:, 0:J], ranks.one_hot[:, bass.ds(g * J, J)], ALU.mult).then_inc(rk_step, 1)
                wait_apart(dve, rk_step, 2 * g + 2, passed)
                v.tensor_copy(seen[:, 0], seen[:, J]).then_inc(rt_step, 1)
                v.tensor_reduce(ranks.rank[:, bass.ds(g * J, J)], mine[:], AX.X, ALU.add).then_inc(rk_step, 1)

            def scale(g, k, i):
                wait(dve, eneg_ok, g + 1)
                v.tensor_scalar(eneg[:], eneg[:], 1.0, None, ALU.add).then_inc(sg_step, 1)
                wait(dve, sg_step, 2 * g + 1)
                v.reciprocal(score[:, k], eneg[:]).then_inc(sg_step, 1)
                wait(dve, sg_step, 2 * g + 2)
                wait(dve, xs_out[k], 16 * i)
                for j in range(J):
                    s = v.tensor_scalar(xs[:, k, j], xn[:, k, j], score[:, k, j:j + 1], None, ALU.mult)
                s.then_inc(xs_ok, 1)

            def mul(g, it):
                wait(dve, u_mm, IT * g + it + 1)
                wait(dve, silu_ok, IT * g + it + 1)
                wait(dve, hlo_ok, IT * (g - 1) + it + 1)
                v.tensor_tensor(h32[:, it], silu[:, it % 2], psU[:, it % 2], ALU.mult).then_inc(h_ok, 1)

            def h_low(g, k, it):
                wait(dve, hhi_ok, IT * g + it + 1)
                v.tensor_tensor(h_lo[k][:, it], h32[:, it], h_hi[k][:, it].bitcast(F32), ALU.subtract).then_inc(hlo_ok, 1)

            stats_of(0, 0, 0)
            norm(0, 0)
            for n in range(3):
                dve.wait_ge(w_hi_ok, n + 1)
                v.tensor_tensor(w_lo[n][:], raw[n], w_hi[n][:].bitcast(F32), ALU.subtract).then_inc(w_ok, 1)
                if n == 0:
                    xT_low(0, 0, 0)
            dve.wait_ge(iota_ok, 1)
            v.tensor_copy(expert_f[:], expert_i[:]).then_inc(rk_step, 1)
            dve.wait_ge(ident_ok, 2)
            v.tensor_copy(keep.ident_bf[:], keep.ident[:])
            v.tensor_copy(keep.mask_bf[:], maskf[:])
            stats_of(1, 1, 0)
            norm(1, 1)

            def pair(i, last):
                for k in range(2):
                    g = 2 * i + k
                    route(g)
                    mul(g, 0)
                    rank(g)
                    h_low(g, k, 0)
                    scale(g, k, i)
                    mul(g, 1)
                    rank_sum(g)
                    h_low(g, k, 1)
                    if not last:
                        stats_of(g + 2, k, i + 1)
                    mul(g, 2)
                    h_low(g, k, 2)
                    if not last:
                        norm(g + 2, k)
                    mul(g, 3)
                    h_low(g, k, 3)
                    if not (last and k == 1):
                        xT_low(g + 1, 1 - k, i + k)
            each_pair(dve, NG // 2, pair)
            dve.wait_ge(rt_step, 1 + RS * NG)
            v.tensor_copy(ranks.here[:], seen[:, 0])

        @block.scalar
        def _(act):
            s = nc.scalar

            def xT_high(g, k, i):
                wait(act, xt_out[k], 32 * i)
                wait(act, u_mm, IT * (g - 1))
                for c in range(C):
                    wait(act, t_mm, C * g + c + 1)
                    s.copy(xT_hi[k][:, c], psT[:, c]).then_inc(xh_ok, 1)

            def logits(g):
                wait(act, lg_mm, g + 1)
                s.copy(lg2[:].rearrange("p j a e -> p j (a e)"), psL).then_inc(lg_ok, 1)

            def silu_of(g, it):
                wait(act, g_mm, IT * g + it + 1)
                wait(act, h_ok, IT * g + it - 1)
                s.activation(silu[:, it % 2], psG[:, it % 2], ACT.Silu).then_inc(silu_ok, 1)

            def h_high(g, k, it):
                wait(act, h_ok, IT * g + it + 1)
                wait(act, d_mm, g - 1)
                s.copy(h_hi[k][:, it], h32[:, it]).then_inc(hhi_ok, 1)

            def shared_out(g, k, i):
                wait(act, d_mm, g + 1)
                wait(act, sh_out[k], 16 * i)
                s.copy(sh[:, k], psD[:]).then_inc(sh_ok, 1)

            xT_high(0, 0, 0)
            for n in range(3):
                act.wait_ge(w_in[n], 16)
                s.copy(w_hi[n][:], raw[n]).then_inc(w_hi_ok, 1)

            def pair(i, last):
                for k in range(2):
                    g = 2 * i + k
                    logits(g)
                    for it in range(IT):
                        silu_of(g, it)
                        if it + 1 < IT:
                            h_high(g, k, it)
                    h_high(g, k, IT - 1)
                    if not (last and k == 1):
                        xT_high(g + 1, 1 - k, i + k)
                    if not is_first(g):
                        shared_out(g - 1, 1 - k, i - 1 + k)
            each_pair(act, NG // 2, pair)
            shared_out(NG - 1, 1, NG // 2 - 1)

        @block.tensor
        def _(pe):
            def transposes(g, k):
                wait(pe, xn_ok, g + 1)
                wait(pe, lg_ok, g)
                wait(pe, xl_ok, C * g)
                for c in range(C):
                    for j in range(J):
                        mm = nc.tensor.transpose(psT[:, c, j * P:(j + 1) * P],
                                                 xn[:, k, j, c * P:(c + 1) * P], keep.ident[:])
                    mm.then_inc(t_mm, 1)

            def logits(g, k):
                wait(pe, xl_ok, C * (g + 1))
                for j in range(J):
                    for c in range(C):
                        nc.tensor.matmul(psL[:, j], xT_hi[k][:, c, j * P:(j + 1) * P],
                                         gate_hl[:, c].rearrange("p a e -> p (a e)"),
                                         start=(j == 0 and c == 0), stop=False, skip_group_check=True)
                    for c in range(C):
                        mm = nc.tensor.matmul(psL[:, j, 0:E], xT_lo[k][:, c, j * P:(j + 1) * P], gate_hl[:, c, 0],
                                              start=False, stop=(c == C - 1), skip_group_check=True)
                mm.then_inc(lg_mm, 1)

            def up(g, k):
                wait(pe, xl_ok, C * (g + 1))
                if is_first(g):
                    pe.wait_ge(w_ok, 2)
                for it in range(IT):
                    cols = slice(it * P, (it + 1) * P)
                    wait(pe, silu_ok, IT * g + it - 1)
                    for c in range(C):
                        mm = split_matmuls(nc, psG[:, it % 2], w_hi[0][:, c, cols], w_lo[0][:, c, cols],
                                           xT_hi[k][:, c], xT_lo[k][:, c], c == 0, c == C - 1)
                    mm.then_inc(g_mm, 1)
                    wait(pe, h_ok, IT * g + it - 1)
                    for c in range(C):
                        mm = split_matmuls(nc, psU[:, it % 2], w_hi[1][:, c, cols], w_lo[1][:, c, cols],
                                           xT_hi[k][:, c], xT_lo[k][:, c], c == 0, c == C - 1)
                    mm.then_inc(u_mm, 1)

            def down(g, k):
                if is_first(g):
                    pe.wait_ge(w_ok, 3)
                wait(pe, sh_ok, g)
                for it in range(IT):
                    wait(pe, hlo_ok, IT * g + it + 1)
                    for j in range(J):
                        cols = slice(j * P, (j + 1) * P)
                        mm = split_matmuls(nc, psD[:, j], h_hi[k][:, it, cols], h_lo[k][:, it, cols],
                                           w_hi[2][:, it], w_lo[2][:, it],
                                           it == 0 and j % 2 == 0, it == IT - 1)
                mm.then_inc(d_mm, 1)

            pe.wait_ge(ident_ok, 1)
            transposes(0, 0)
            pe.wait_ge(gate_ok, 2)
            logits(0, 0)

            def pair(i, last):
                for k in range(2):
                    g = 2 * i + k
                    up(g, k)
                    if not (last and k == 1):
                        transposes(g + 1, 1 - k)
                    if not is_first(g):
                        down(g - 1, 1 - k)
                    if not (last and k == 1):
                        logits(g + 1, 1 - k)
            each_pair(pe, NG // 2, pair)
            down(NG - 1, 1)


def routing_stage(nc, W_qkv, d_t, keep, ranks, D, E, NT, ET):
    NC = keep.slot_token.shape[1]
    TT = keep.tile_expert.shape[1]
    C = D // P
    with ExitStack() as st:
        def sb(name, shape, dt=F32):
            return st.enter_context(nc.sbuf_tensor("r_" + name, shape, dt))

        def sem(name):
            return st.enter_context(nc.semaphore("r_" + name))

        nothing = sb("nothing", [P, ST // P, D])
        wqkv = sb("wqkv", [P, C, 3 * D])
        wT = sb("wT", [P, 2 * C, D])
        a32 = sb("a32", [P, C, D])
        zeros = sb("zeros", [P, E])
        counts = sb("counts", [P, 2, E])
        tiles_i = sb("tiles_i", [P, E], I32)
        tiles_s = sb("tiles_s", [P, E], I32)
        tiles = sb("tiles", [P, E])
        tiles_cum = sb("tiles_cum", [P, E])
        base = sb("base", [P, E])
        shift = sb("shift", [P, E])
        moved = sb("moved", [P, NT, E])
        start = sb("start", [P, NT])
        pos = sb("pos", [P, NT])
        pos_i = sb("pos_i", [P, NT], I32)
        lo_i = sb("lo_i", [P, NT], I32)
        hi_i = sb("hi_i", [P, NT], I32)
        lo = sb("lo", [P, NT])
        hi = sb("hi", [P, NT])
        col_i = sb("col_i", [P, max(NC, P)], I32)
        token_i = sb("token_i", [P, NT], I32)
        col = sb("col", [P, max(NC, P)])
        token = sb("token", [P, NT])
        below = sb("below", [P, P])
        ones = sb("ones", [P, P])
        lo_hot = sb("lo_hot", [P, 2, P])
        hi_hot = sb("hi_hot", [P, 2, NC])
        past = sb("past", [1, TT, E])
        tile_f = sb("tile_f", [1, TT])
        used = sb("used", [1, 1], I32)
        psC = st.enter_context(nc.psum_tensor("r_psC", [P, 2, E], F32))
        psS = st.enter_context(nc.psum_tensor("r_psS", [P, 512], F32))
        psT = st.enter_context(nc.psum_tensor("r_psT", [P, 2 * C, D], F32))
        psA = st.enter_context(nc.psum_tensor("r_psA", [P, C, 2 * D], F32))
        zero_ok, zero_out = sem("zero_ok"), sem("zero_out")
        consts, c_mm, step, hot_ok, s_mm, w_in, wt_mm, wt_ok, a_mm, a_ok, split_ok = (
            sem(n) for n in ("consts", "c_mm", "step", "hot_ok", "s_mm", "w_in",
                             "wt_mm", "wt_ok", "a_mm", "a_ok", "split_ok"))
        block = st.enter_context(nc.Block())

        @block.sync
        def _(sp):
            sp.dma_start(wqkv[:], W_qkv.rearrange("(c p) n -> p c n", p=P)).then_inc(w_in, 16)
            sp.wait_ge(zero_ok, 1)
            with sp.Fori(NT * P // ST, ET) as t:
                sp.dma_start(d_t[t], nothing[:]).then_inc(zero_out, 16)
            sp.wait_ge(zero_out, 16 * (ET - NT * P // ST))

        @block.gpsimd
        def _(pool):
            g = nc.gpsimd
            g.memset(nothing[:], 0.0).then_inc(zero_ok, 1)
            g.memset(ones[:], 1.0).then_inc(consts, 1)
            pool.wait_ge(consts, 1)
            g.affine_select(out=below[:], in_=ones[:], compare_op=ALU.is_gt, fill=0.0,
                            base=0, pattern=[[1, P]], channel_multiplier=-1).then_inc(consts, 1)
            g.iota(col_i[:], pattern=[[1, col_i.shape[1]]], base=0, channel_multiplier=0).then_inc(consts, 1)
            g.iota(token_i[:], pattern=[[P, NT]], base=0, channel_multiplier=1).then_inc(consts, 1)
            pool.wait_ge(split_ok, 1)
            g.tensor_tensor(keep.v_lo[:], wqkv[:, :, 2 * D:3 * D], keep.v_hi[:].bitcast(F32), ALU.subtract)
            pool.wait_ge(split_ok, 2)
            g.tensor_tensor(keep.a_lo[:], a32[:], keep.a_hi[:].bitcast(F32), ALU.subtract)

        @block.scalar
        def _(act):
            s = nc.scalar
            act.wait_ge(w_in, 16)
            s.copy(keep.v_hi[:], wqkv[:, :, 2 * D:3 * D]).then_inc(split_ok, 1)
            act.wait_ge(wt_mm, 1)
            s.copy(wT[:], psT[:]).then_inc(wt_ok, 1)
            act.wait_ge(a_mm, 1)
            s.mul(a32[:], psA[:, :, 0:D], float(D) ** -0.5).then_inc(a_ok, 1)
            act.wait_ge(a_ok, 1)
            s.copy(keep.a_hi[:], a32[:]).then_inc(split_ok, 1)

        @block.vector
        def _(dve):
            v = nc.vector
            n = [0]

            def done(ins):
                n[0] += 1
                ins.then_inc(step, 1)
                dve.wait_ge(step, n[0])

            v.memset(zeros[:], 0.0)
            dve.wait_ge(c_mm, 1)
            done(v.tensor_copy(counts[:], psC[:]))
            done(v.tensor_scalar(tiles_i[:], counts[:, 1], float(ST - 1), None, ALU.add))
            done(v.tensor_scalar(tiles_s[:], tiles_i[:], ST.bit_length() - 1, None, ALU.arith_shift_right))
            done(v.tensor_copy(tiles[:], tiles_s[:]))
            done(v.tensor_tensor_scan(tiles_cum[:], zeros[:], tiles[:], 0.0, ALU.add, ALU.add))
            done(v.tensor_tensor(base[:], tiles_cum[:], tiles[:], ALU.subtract))
            done(v.scalar_tensor_tensor(out=shift[:], in0=base[:], scalar=float(ST), in1=counts[:, 0],
                                        op0=ALU.mult, op1=ALU.add))
            done(v.tensor_tensor(moved[:], ranks.one_hot[:], shift[:].unsqueeze(1).to_broadcast([P, NT, E]), ALU.mult))
            done(v.tensor_reduce(start[:], moved[:], AX.X, ALU.add))
            done(v.tensor_tensor(pos[:], start[:], ranks.rank[:], ALU.add))
            done(v.tensor_copy(pos_i[:], pos[:]))
            v.tensor_scalar(hi_i[:], pos_i[:], P.bit_length() - 1, None, ALU.arith_shift_right)
            done(v.tensor_scalar(lo_i[:], pos_i[:], P - 1, None, ALU.bitwise_and))
            dve.wait_ge(consts, 4)
            v.tensor_copy(col[:], col_i[:])
            v.tensor_copy(token[:], token_i[:])
            v.tensor_copy(hi[:], hi_i[:])
            done(v.tensor_copy(lo[:], lo_i[:]))

            def spread(i, last):
                for k in range(2):
                    t = 2 * i + k
                    wait(dve, s_mm, t - 1)
                    v.tensor_scalar(lo_hot[:, k], col[:, 0:P], lo[:, bass.ds(t, 1)], None, ALU.is_equal)
                    v.tensor_scalar(hi_hot[:, k], col[:, 0:NC], hi[:, bass.ds(t, 1)], token[:, bass.ds(t, 1)],
                                    ALU.is_equal, ALU.mult).then_inc(hot_ok, 1)
            each_pair(dve, NT // 2, spread)

            v.tensor_copy(keep.position[:], pos_i[:])
            done(v.tensor_tensor(past[:], tiles_cum[0:1].unsqueeze(1).to_broadcast([1, TT, E]),
                                 col[0:1, 0:TT].unsqueeze(2).to_broadcast([1, TT, E]), ALU.is_le))
            done(v.tensor_reduce(tile_f[:], past[:], AX.X, ALU.add))
            done(v.tensor_scalar(tile_f[:], tile_f[:], float(E - 1), None, ALU.min))
            v.tensor_copy(keep.tile_expert[:], tile_f[:])
            done(v.tensor_copy(used[:], tiles_cum[0:1, E - 1:E]))
            v.tensor_scalar(keep.half_tiles[:], used[:], 1, None, ALU.arith_shift_right)
            dve.wait_ge(s_mm, NT)
            v.tensor_copy(keep.slot_token[:], psS[:, 0:NC])

        @block.tensor
        def _(pe):
            pe.wait_ge(consts, 2)
            nc.tensor.matmul(psC[:, 0], below[:], ranks.here[:], start=True, stop=True)
            nc.tensor.matmul(psC[:, 1], ones[:], ranks.here[:], start=True, stop=True).then_inc(c_mm, 1)
            pe.wait_ge(w_in, 16)
            for w in range(2):
                for e in range(C):
                    for c in range(C):
                        mm = nc.tensor.transpose(psT[:, w * C + e, c * P:(c + 1) * P],
                                                 wqkv[:, c, w * D + e * P:w * D + (e + 1) * P], keep.ident[:])
            mm.then_inc(wt_mm, 1)
            pe.wait_ge(wt_ok, 1)
            for c in range(C):
                for e in range(C):
                    mm = nc.tensor.matmul(psA[:, c, 0:D], wT[:, e, c * P:(c + 1) * P], wT[:, C + e, :],
                                          start=(e == 0), stop=(e == C - 1))
            mm.then_inc(a_mm, 1)

            def gather(i, last):
                for k in range(2):
                    t = 2 * i + k
                    wait(pe, hot_ok, t + 1)
                    nc.tensor.matmul(psS[:, 0:NC], lo_hot[:, k], hi_hot[:, k], start=is_first(t),
                                     stop=(last and k == 1), skip_group_check=True).then_inc(s_mm, 1)
            each_pair(pe, NT // 2, gather)


def expert_stage(nc, xs, rgw, ruw, rdw, d_t, keep, D, F, E, ET):
    C, H, IT = D // P, ST // P, F // P
    Q = IT // 2
    with ExitStack() as st:
        def sb(name, shape, dt=F32):
            return st.enter_context(nc.sbuf_tensor("e_" + name, shape, dt))

        def ps(name, shape):
            return st.enter_context(nc.psum_tensor("e_" + name, shape, F32))

        def sem(name):
            return st.enter_context(nc.semaphore("e_" + name))

        raw = [sb(f"raw{k}", [P, 3, C * F]) for k in range(2)]
        whi = [sb(f"whi{k}", [P, 3, C * F], F32R) for k in range(2)]
        wlo = [sb(f"wlo{k}", [P, 3, C * F], F32R) for k in range(2)]
        slot = sb("slot", [P, 2, H], I32)
        xg = sb("xg", [P, 2, H, D])
        x_hi = sb("x_hi", [P, 2, C, ST], F32R)
        x_lo = sb("x_lo", [P, 2, C, ST], F32R)
        silu = sb("silu", [P, 2, 2 * ST])
        h32 = sb("h32", [P, 2, 2 * ST])
        h_hi = [sb(f"h_hi{k}", [P, Q, 2 * ST], F32R) for k in range(2)]
        h_lo = [sb(f"h_lo{k}", [P, Q, 2 * ST], F32R) for k in range(2)]
        dout = sb("dout", [P, 2, H, D])
        psT = ps("psT", [P, C, ST])
        psG = ps("psG", [P, 2, 2, ST])
        psU = ps("psU", [P, 2, 2, ST])
        psD = ps("psD", [P, H, D])
        w_in = [sem(f"w_in{k}") for k in range(2)]
        x_in = [sem(f"x_in{k}") for k in range(2)]
        d_out = [sem(f"d_out{k}") for k in range(2)]
        passed = sem("passed")
        slot_ok, t_mm, xh_ok, xl_ok = (sem(n) for n in ("slot_ok", "t_mm", "xh_ok", "xl_ok"))
        whi_ok, whd_ok, wlo_ok = (sem(n) for n in ("whi_ok", "whd_ok", "wlo_ok"))
        g_mm, u_mm, silu_ok, h_ok, hhi_ok, hlo_ok, d_mm, do_ok = (
            sem(n) for n in ("g_mm", "u_mm", "silu_ok", "h_ok", "hhi_ok", "hlo_ok", "d_mm", "do_ok"))
        block = st.enter_context(nc.Block())

        def part(w, k, n):
            v = w[k][:, n]
            return v.rearrange("p (c f) -> p c f", c=C) if n < 2 else v.rearrange("p (i d) -> p i d", i=IT)

        def tiles(eng, body):
            R = eng.value_load(keep.half_tiles[0:1, 0:1], min_val=1, max_val=ET // 2 - 1)
            for i in range(2):
                for k in range(2):
                    body(2 * i + k, k, i)
            with eng.Fori(2, ET // 2) as i:
                with eng.If(i < R + 1):
                    for k in range(2):
                        body(2 * i + k, k, i)
            return R

        @block.sync
        def _(sp):
            def load(t, k):
                wait_apart(sp, whi_ok, 2 * (t - 1), passed)
                wait_apart(sp, whd_ok, t - 1, passed)
                wait_apart(sp, wlo_ok, 3 * (t - 1), passed)
                e = sp.value_load(keep.tile_expert[0:1, bass.ds(t, 1)], min_val=0, max_val=E - 1)
                sp.dma_start(part(raw, k, 0), rgw[e].rearrange("(c p) f -> p c f", p=P)).then_inc(w_in[k], 16)
                sp.dma_start(part(raw, k, 1), ruw[e].rearrange("(c p) f -> p c f", p=P)).then_inc(w_in[k], 16)
                sp.dma_start(part(raw, k, 2), rdw[e].rearrange("(i p) d -> p i d", p=P)).then_inc(w_in[k], 16)

            def store(t, k):
                wait(sp, do_ok, t + 1)
                sp.dma_start(d_t[t], dout[:, k]).then_inc(d_out[k], 16)

            load(0, 0)
            load(1, 1)

            def step(t, k, i):
                load(t + 2, k)
                if not is_first(t):
                    store(t - 1, 1 - k)
            R = tiles(sp, step)
            for k in range(2):
                wait_apart(sp, w_in[k], (R + 2) * 48, passed)
                wait_apart(sp, d_out[k], (R + (1 - k)) * 16, passed)

        @block.gpsimd
        def _(pool):
            g = nc.gpsimd

            def gather(t, k, i):
                wait_apart(pool, x_in[k], 16 * H * i, passed)
                g.tensor_copy(slot[:, k], keep.slot_token[:, bass.ds(t * H, H)]).then_inc(slot_ok, 1)
                wait(pool, t_mm, t - 1)
                wait_apart(pool, slot_ok, t + 1, passed)
                for h in range(H):
                    g.indirect_dma_start(out=xg[:, k, h], out_offset=None, in_=xs,
                                         in_offset=bass.IndirectOffsetOnAxis(slot[:, k, h:h + 1], 0)).then_inc(x_in[k], 16)

            def high_down(t, k, i):
                wait(pool, d_mm, t - 1)
                wait_apart(pool, w_in[k], 48 * (i + 1), passed)
                g.tensor_copy(whi[k][:, 2], raw[k][:, 2]).then_inc(whd_ok, 1)

            gather(0, 0, 0)
            gather(1, 1, 0)
            high_down(0, 0, 0)

            def step(t, k, i):
                gather(t + 2, k, i + 1)
                high_down(t + 1, 1 - k, i + k)
            R = tiles(pool, step)
            for k in range(2):
                wait_apart(pool, x_in[k], (R + 2) * (16 * H), passed)

        @block.vector
        def _(dve):
            v = nc.vector

            def low(t, k, n):
                if n < 2:
                    wait(dve, whi_ok, 2 * t + n + 1)
                else:
                    wait(dve, whd_ok, t + 1)
                wait(dve, d_mm if n == 2 else u_mm, (t - 1) * (1 if n == 2 else Q))
                v.tensor_tensor(wlo[k][:, n], raw[k][:, n], whi[k][:, n].bitcast(F32), ALU.subtract).then_inc(wlo_ok, 1)

            def x_low(t, k):
                wait(dve, xh_ok, t + 1)
                v.tensor_tensor(x_lo[:, k], psT[:], x_hi[:, k].bitcast(F32), ALU.subtract).then_inc(xl_ok, 1)

            def mul(t, q):
                wait(dve, u_mm, Q * t + q + 1)
                wait(dve, silu_ok, Q * t + q + 1)
                wait(dve, hlo_ok, Q * (t - 1) + q + 1)
                v.tensor_tensor(h32[:, q], silu[:, q], psU[:, q].rearrange("p a n -> p (a n)"), ALU.mult).then_inc(h_ok, 1)

            def h_low(t, k, q):
                wait(dve, hhi_ok, Q * t + q + 1)
                v.tensor_tensor(h_lo[k][:, q], h32[:, q], h_hi[k][:, q].bitcast(F32), ALU.subtract).then_inc(hlo_ok, 1)

            for n in range(3):
                low(0, 0, n)
            x_low(0, 0)

            def step(t, k, i):
                mul(t, 0)
                low(t + 1, 1 - k, 0)
                h_low(t, k, 0)
                mul(t, 1)
                low(t + 1, 1 - k, 1)
                h_low(t, k, 1)
                x_low(t + 1, 1 - k)
                low(t + 1, 1 - k, 2)
            tiles(dve, step)

        @block.scalar
        def _(act):
            s = nc.scalar

            def high(t, k, i, n):
                if n == 0:
                    wait(act, w_in[k], 48 * (i + 1))
                    wait(act, u_mm, Q * (t - 1))
                s.copy(whi[k][:, n], raw[k][:, n]).then_inc(whi_ok, 1)

            def x_high(t, k):
                wait(act, t_mm, t + 1)
                s.copy(x_hi[:, k], psT[:]).then_inc(xh_ok, 1)

            def silu_of(t, q):
                wait(act, g_mm, Q * t + q + 1)
                wait(act, h_ok, Q * (t - 1) + q + 1)
                s.activation(silu[:, q], psG[:, q].rearrange("p a n -> p (a n)"), ACT.Silu).then_inc(silu_ok, 1)

            def h_high(t, k, q):
                wait(act, h_ok, Q * t + q + 1)
                s.copy(h_hi[k][:, q], h32[:, q]).then_inc(hhi_ok, 1)

            def d_copy(t, k, i):
                wait(act, d_mm, t + 1)
                wait(act, d_out[k], 16 * i)
                s.copy(dout[:, k], psD[:]).then_inc(do_ok, 1)

            high(0, 0, 0, 0)
            high(0, 0, 0, 1)
            x_high(0, 0)

            def step(t, k, i):
                silu_of(t, 0)
                high(t + 1, 1 - k, i + k, 0)
                h_high(t, k, 0)
                silu_of(t, 1)
                high(t + 1, 1 - k, i + k, 1)
                h_high(t, k, 1)
                x_high(t + 1, 1 - k)
                if not is_first(t):
                    d_copy(t - 1, 1 - k, i - 1 + k)
            tiles(act, step)

        @block.tensor
        def _(pe):
            def transposes(t, k, i):
                wait(pe, x_in[k], 16 * H * (i + 1))
                wait(pe, xl_ok, t)
                for c in range(C):
                    for h in range(H):
                        mm = nc.tensor.transpose(psT[:, c, h * P:(h + 1) * P], xg[:, k, h, c * P:(c + 1) * P], keep.ident[:])
                mm.then_inc(t_mm, 1)

            def up(t, k):
                wait(pe, xl_ok, t + 1)
                for q in range(Q):
                    for n, (psum, freed, out) in enumerate(((psG, silu_ok, g_mm), (psU, h_ok, u_mm))):
                        wait(pe, wlo_ok, 3 * t + n + 1)
                        wait(pe, freed, Q * (t - 1) + q + 1)
                        for a in range(2):
                            cols = slice((2 * q + a) * P, (2 * q + a + 1) * P)
                            for c in range(C):
                                mm = split_matmuls(nc, psum[:, q, a], part(whi, k, n)[:, c, cols], part(wlo, k, n)[:, c, cols],
                                                   x_hi[:, k, c], x_lo[:, k, c], c == 0, c == C - 1)
                        mm.then_inc(out, 1)

            def down(t, k):
                wait(pe, wlo_ok, 3 * t + 3)
                wait(pe, do_ok, t)
                for it in range(IT):
                    wait(pe, hlo_ok, Q * t + it // 2 + 1)
                    for h in range(H):
                        cols = slice((it % 2) * ST + h * P, (it % 2) * ST + (h + 1) * P)
                        mm = split_matmuls(nc, psD[:, h], h_hi[k][:, it // 2, cols], h_lo[k][:, it // 2, cols],
                                           part(whi, k, 2)[:, it], part(wlo, k, 2)[:, it],
                                           it == 0 and h == 0, it == IT - 1)
                mm.then_inc(d_mm, 1)

            transposes(0, 0, 0)

            def step(t, k, i):
                up(t, k)
                transposes(t + 1, 1 - k, i + k)
                if not is_first(t):
                    down(t - 1, 1 - k)
            tiles(pe, step)


def attention_stage(nc, x_g, sh_g, d_rows, xth_g, xtl_g, out_g, keep, D, B, N):
    C, NB, GB = D // P, N // P, N // GT
    J = GT // P
    QU = C * GB
    VU = NB // 2
    groups = [i // 4 + 1 for i in range(NB)]
    before = [sum(groups[:i]) for i in range(NB + 1)]
    TG = before[NB]
    assert TG % 4 == 0 and NB % 2 == 0
    with ExitStack() as st:
        def sb(name, shape, dt=F32):
            return st.enter_context(nc.sbuf_tensor("t_" + name, shape, dt))

        def ps(name, shape):
            return st.enter_context(nc.psum_tensor("t_" + name, shape, F32))

        def sem(name):
            return st.enter_context(nc.semaphore("t_" + name))

        x_hi = [sb(f"x_hi{k}", [P, C, N], F32R) for k in range(2)]
        x_lo = [sb(f"x_lo{k}", [P, C, N], F32R) for k in range(2)]
        q_hi = sb("q_hi", [P, C, N], F32R)
        q_lo = sb("q_lo", [P, C, N], F32R)
        v_hi = sb("v_hi", [P, NB, D], F32R)
        v_lo = sb("v_lo", [P, NB, D], F32R)
        prob = [sb(f"prob{k}", [P, N]) for k in range(2)]
        pT_hi = [sb(f"pT_hi{k}", [P, 4, P], F32R) for k in range(4)]
        pT_lo = [sb(f"pT_lo{k}", [P, 4, P], F32R) for k in range(4)]
        xr = sb("xr", [P, 2, J, D])
        shr = sb("shr", [P, 2, J, D])
        pos = sb("pos", [P, 2, 1], I32)
        routed = sb("routed", [P, 2, D])
        sum1 = sb("sum1", [P, 2, D])
        base = sb("base", [P, 2, D])
        negmax = sb("negmax", [P, 2])
        rowsum = sb("rowsum", [P, 2])
        rinv = sb("rinv", [P, 2])
        outb = sb("outb", [P, 2, D])
        psS = ps("psS", [P, 4, 512])
        psT = ps("psT", [P, 2, 4, P])
        psO = ps("psO", [P, 2, 512])
        x_in = [sem(f"x_in{k}") for k in range(2)]
        r_in = [sem(f"r_in{k}") for k in range(2)]
        d_in = [sem(f"d_in{k}") for k in range(2)]
        o_out = [sem(f"o_out{k}") for k in range(2)]
        q_mm, qh_ok, ql_ok, v_mm, vh_ok, vl_ok = (sem(n) for n in ("q_mm", "qh_ok", "ql_ok", "v_mm", "vh_ok", "vl_ok"))
        s_mm, max_ok, exp_ok, t_mm, ph_ok, pl_ok, pv_mm, o_ok, rinv_ok = (
            sem(n) for n in ("s_mm", "max_ok", "exp_ok", "t_mm", "ph_ok", "pl_ok", "pv_mm", "o_ok", "rinv_ok"))
        passed = sem("passed")
        pos_ok, sum_ok, base_ok = (sem(n) for n in ("pos_ok", "sum_ok", "base_ok"))
        block = st.enter_context(nc.Block())

        def width(i):
            n = (i + 1) * P
            return [min(512, -(-(n - c) // 256) * 256) for c in range(0, n, 512)]

        @block.sync
        def _(sp):
            def load_xt(b, k):
                wait(sp, s_mm, NB * (b - 1))
                for g in range(GB):
                    cols = slice(g * GT, (g + 1) * GT)
                    sp.dma_start(x_hi[k][:, :, cols].bitcast(F32), xth_g[b * GB + g]).then_inc(x_in[k], 16)
                    sp.dma_start(x_lo[k][:, :, cols].bitcast(F32), xtl_g[b * GB + g]).then_inc(x_in[k], 16)

            def load_rows(n, k):
                wait(sp, base_ok, J * (n - 1))
                sp.dma_start(xr[:, k], x_g[n]).then_inc(r_in[k], 16)
                sp.dma_start(shr[:, k], sh_g[n]).then_inc(r_in[k], 16)

            load_xt(0, 0)
            load_rows(0, 0)
            load_rows(1, 1)
            load_xt(1, 1)

            def pair(i, last):
                for k in range(2):
                    b = 2 * i + k
                    for g in range(GB):
                        for j in range(J):
                            r = b * NB + g * J + j
                            wait(sp, o_ok, r + 1)
                            sp.dma_start(out_g[b * GB + g][:, j], outb[:, j % 2]).then_inc(o_out[j % 2], 16)
                        if not (last and k == 1 and g >= GB - 2):
                            load_rows(b * GB + g + 2, g % 2)
                    if not last:
                        load_xt(b + 2, k)
            each_pair(sp, B // 2, pair)
            for k in range(2):
                sp.wait_ge(o_out[k], 16 * (B * NB // 2))

        @block.gpsimd
        def _(pool):
            g = nc.gpsimd

            def gather(r, k, n):
                wait(pool, sum_ok, r - 1)
                wait_apart(pool, d_in[k], 16 * n, passed)
                g.tensor_copy(pos[:, k], keep.position[:, bass.ds(r, 1)]).then_inc(pos_ok, 1)
                wait_apart(pool, pos_ok, r + 1, passed)
                g.indirect_dma_start(out=routed[:, k], out_offset=None, in_=d_rows,
                                     in_offset=bass.IndirectOffsetOnAxis(pos[:, k, 0:1], 0)).then_inc(d_in[k], 16)

            gather(0, 0, 0)
            gather(1, 1, 0)

            def pair(i, last):
                for t in range(2 * NB):
                    r = i * 2 * NB + t
                    k, kg, j = t % 2, (t // J) % 2, t % J
                    if j == 0:
                        wait(pool, r_in[kg], 32 * (i * GB + t // (2 * J) + 1))
                    wait(pool, d_in[k], 16 * (i * NB + t // 2 + 1))
                    wait(pool, o_ok, r - 1)
                    g.tensor_tensor(sum1[:, k], routed[:, k], shr[:, kg, j], ALU.add).then_inc(sum_ok, 1)
                    wait(pool, sum_ok, r + 1)
                    g.tensor_tensor(base[:, k], sum1[:, k], xr[:, kg, j], ALU.add).then_inc(base_ok, 1)
                    if not (last and t >= 2 * NB - 2):
                        gather(r + 2, k, i * NB + t // 2 + 1)
            each_pair(pool, B // 2, pair)

        @block.vector
        def _(dve):
            v = nc.vector

            def q_low(b, u):
                wait(dve, qh_ok, QU * b + u + 1)
                c, n = u % C, u // C
                v.tensor_tensor(q_lo[:, c, n * 512:(n + 1) * 512], psS[:, u % 4],
                                q_hi[:, c, n * 512:(n + 1) * 512].bitcast(F32), ALU.subtract).then_inc(ql_ok, 1)

            def v_low(b, u):
                wait(dve, vh_ok, VU * b + u + 1)
                v.tensor_tensor(v_lo[:, 2 * u:2 * u + 2].rearrange("p a d -> p (a d)"), psS[:, u % 4],
                                v_hi[:, 2 * u:2 * u + 2].rearrange("p a d -> p (a d)").bitcast(F32),
                                ALU.subtract).then_inc(vl_ok, 1)

            def row_max(b, i):
                r = b * NB + i
                wait(dve, s_mm, r + 1)
                wait(dve, exp_ok, r - 1)
                v.tensor_reduce(negmax[:, i % 2:i % 2 + 1], psS[:].rearrange("p a n -> p (a n)")[:, 0:(i + 1) * P],
                                AX.X, ALU.max, negate=True).then_inc(max_ok, 1)

            def p_low(b, i, q):
                n = b * TG + before[i] + q
                s = (before[i] + q) % 4
                m = min(4, i + 1 - 4 * q)
                wait(dve, ph_ok, n + 1)
                v.tensor_tensor(pT_lo[s][:, 0:m], psT[:, s % 2, 0:m], pT_hi[s][:, 0:m].bitcast(F32),
                                ALU.subtract).then_inc(pl_ok, 1)

            def output(b, i, half):
                r = b * NB + i
                k = i % 2
                v.reciprocal(rinv[:, k:k + 1], rowsum[:, k:k + 1]).then_inc(rinv_ok, 1)
                wait(dve, rinv_ok, r + 1)
                wait(dve, pv_mm, b * TG + before[i + 1])
                wait(dve, base_ok, r + 1)
                wait(dve, o_out[k], 16 * half)
                v.scalar_tensor_tensor(out=outb[:, k], in0=psO[:, k, 0:D], scalar=rinv[:, k:k + 1], in1=base[:, k],
                                       op0=ALU.mult, op1=ALU.add).then_inc(o_ok, 1)

            for u in range(QU):
                q_low(0, u)

            def pair(p, last):
                for k in range(2):
                    b = 2 * p + k
                    for u in range(VU):
                        v_low(b, u)
                    row_max(b, 0)
                    for i in range(NB):
                        for q in range(min(2, groups[i])):
                            p_low(b, i, q)
                        if i + 1 < NB:
                            row_max(b, i + 1)
                        elif not (last and k == 1):
                            for u in range(QU // 2):
                                q_low(b + 1, u)
                        for q in range(2, groups[i]):
                            p_low(b, i, q)
                        if i + 1 == NB and not (last and k == 1):
                            for u in range(QU // 2, QU):
                                q_low(b + 1, u)
                        output(b, i, b * (NB // 2) + i // 2)
            each_pair(dve, B // 2, pair)

        @block.scalar
        def _(act):
            s = nc.scalar

            def q_high(b, u):
                c, n = u % C, u // C
                wait(act, q_mm, QU * b + u + 1)
                s.copy(q_hi[:, c, n * 512:(n + 1) * 512], psS[:, u % 4]).then_inc(qh_ok, 1)

            def v_high(b, u):
                wait(act, v_mm, VU * b + u + 1)
                s.copy(v_hi[:, 2 * u:2 * u + 2].rearrange("p a d -> p (a d)"), psS[:, u % 4]).then_inc(vh_ok, 1)

            def exp(b, i):
                r = b * NB + i
                wait(act, max_ok, r + 1)
                wait(act, o_ok, r - 1)
                s.activation(prob[i % 2][:, 0:(i + 1) * P], psS[:].rearrange("p a n -> p (a n)")[:, 0:(i + 1) * P],
                             ACT.Exp, bias=negmax[:, i % 2:i % 2 + 1], accum_out=rowsum[:, i % 2:i % 2 + 1]).then_inc(exp_ok, 1)

            def p_high(b, i, q):
                n = b * TG + before[i] + q
                t = (before[i] + q) % 4
                m = min(4, i + 1 - 4 * q)
                wait(act, t_mm, n + 1)
                wait(act, pv_mm, n - 3)
                s.copy(pT_hi[t][:, 0:m], psT[:, t % 2, 0:m]).then_inc(ph_ok, 1)

            for u in range(QU):
                q_high(0, u)

            def pair(p, last):
                for k in range(2):
                    b = 2 * p + k
                    for u in range(VU):
                        v_high(b, u)
                    exp(b, 0)
                    for i in range(NB):
                        for q in range(min(3, groups[i])):
                            p_high(b, i, q)
                            if q == 1 and i + 1 == NB and not (last and k == 1):
                                for u in range(QU // 2):
                                    q_high(b + 1, u)
                        for q in range(3, groups[i]):
                            p_high(b, i, q)
                        if i + 1 < NB:
                            exp(b, i + 1)
                        elif not (last and k == 1):
                            for u in range(QU // 2, QU):
                                q_high(b + 1, u)
            each_pair(act, B // 2, pair)

        @block.tensor
        def _(pe):
            def queries(b, k, u):
                c, n = u % C, u // C
                if u == 0:
                    wait(pe, x_in[k], 32 * GB * (b // 2 + 1) if isinstance(b, int) else 16 * GB * (b - k + 2))
                wait(pe, exp_ok, NB * b)
                if u >= 4:
                    wait(pe, ql_ok, QU * b + u - 3)
                for d in range(C):
                    mm = split_matmuls(nc, psS[:, u % 4], keep.a_hi[:, d, c * P:(c + 1) * P], keep.a_lo[:, d, c * P:(c + 1) * P],
                                       x_hi[k][:, d, n * 512:(n + 1) * 512], x_lo[k][:, d, n * 512:(n + 1) * 512],
                                       d == 0, d == C - 1)
                mm.then_inc(q_mm, 1)

            def values(b, k, u):
                if u < 4:
                    wait(pe, ql_ok, QU * (b + 1) - 3 + u)
                else:
                    wait(pe, vl_ok, VU * b + u - 3)
                for a in range(2):
                    cols = slice((2 * u + a) * P, (2 * u + a + 1) * P)
                    for d in range(C):
                        mm = split_matmuls(nc, psS[:, u % 4, a * D:(a + 1) * D], x_hi[k][:, d, cols], x_lo[k][:, d, cols],
                                           keep.v_hi[:, d], keep.v_lo[:, d], d == 0, d == C - 1)
                mm.then_inc(v_mm, 1)

            def scores(b, k, i):
                if i == 0:
                    wait(pe, vl_ok, VU * (b + 1))
                wait(pe, exp_ok, b * NB + i)
                rows = slice(i * P, (i + 1) * P)
                for n, w in enumerate(width(i)):
                    diagonal = n == i // 4
                    for d in range(C):
                        split_matmuls(nc, psS[:, n, 0:w], q_hi[:, d, rows], q_lo[:, d, rows],
                                      x_hi[k][:, d, n * 512:n * 512 + w], x_lo[k][:, d, n * 512:n * 512 + w],
                                      d == 0, d == C - 1 and not diagonal)
                mm = nc.tensor.matmul(psS[:, i // 4, (i % 4) * P:(i % 4 + 1) * P], keep.ident_bf[:], keep.mask_bf[:],
                                      start=False, stop=True, skip_group_check=True)
                mm.then_inc(s_mm, 1)

            def transposes(b, i, q):
                n = b * TG + before[i] + q
                s = (before[i] + q) % 2
                if q == 0:
                    wait(pe, exp_ok, b * NB + i + 1)
                wait(pe, pl_ok, n - 1)
                for m in range(4 * q, min(4 * q + 4, i + 1)):
                    mm = nc.tensor.transpose(psT[:, s, m % 4], prob[i % 2][:, m * P:(m + 1) * P], keep.ident[:])
                mm.then_inc(t_mm, 1)

            def weigh(b, i, q):
                n = b * TG + before[i] + q
                s = (before[i] + q) % 4
                wait(pe, pl_ok, n + 1)
                if q == 0:
                    wait(pe, o_ok, b * NB + i - 1)
                for m in range(4 * q, min(4 * q + 4, i + 1)):
                    mm = split_matmuls(nc, psO[:, i % 2, 0:D], pT_hi[s][:, m % 4], pT_lo[s][:, m % 4],
                                       v_hi[:, m], v_lo[:, m], m == 0, m == i)
                mm.then_inc(pv_mm, 1)

            for u in range(QU):
                queries(0, 0, u)

            def pair(p, last):
                for k in range(2):
                    b = 2 * p + k
                    for u in range(VU):
                        values(b, k, u)
                    scores(b, k, 0)
                    for i in range(NB):
                        for q in range(min(2, groups[i])):
                            transposes(b, i, q)
                        more = not (last and k == 1)
                        if i + 1 < NB:
                            scores(b, k, i + 1)
                        elif more:
                            for u in range(QU // 2):
                                queries(b + 1, 1 - k, u)
                        for q in range(groups[i]):
                            weigh(b, i, q)
                            if q + 2 < groups[i]:
                                transposes(b, i, q + 2)
                        if i + 1 == NB and more:
                            for u in range(QU // 2, QU):
                                queries(b + 1, 1 - k, u)
            each_pair(pe, B // 2, pair)


class Keep:

    def __init__(self, nc, ctx, D, E, NT, SC, ET):
        def sb(name, shape, dt):
            return ctx.enter_context(nc.sbuf_tensor("keep_" + name, shape, dt))

        C = D // P
        self.ident = sb("ident", [P, P], F32)
        self.ident_bf = sb("ident_bf", [P, P], BF16)
        self.mask_bf = sb("mask_bf", [P, P], BF16)
        self.a_hi = sb("a_hi", [P, C, D], F32R)
        self.a_lo = sb("a_lo", [P, C, D], F32R)
        self.v_hi = sb("v_hi", [P, C, D], F32R)
        self.v_lo = sb("v_lo", [P, C, D], F32R)
        self.neghalf = sb("neghalf", [P, GT // P], F32)
        self.euler = sb("euler", [P, GT // P], F32)
        self.position = sb("position", [P, NT], I32)
        self.slot_token = sb("slot_token", [P, SC], I32)
        self.tile_expert = sb("tile_expert", [1, ET + 2], I32)
        self.half_tiles = sb("half_tiles", [1, 1], I32)


class Ranks:

    def __init__(self, nc, ctx, E, NT):
        def sb(name, shape):
            return ctx.enter_context(nc.sbuf_tensor("ranks_" + name, shape, F32))

        self.one_hot = sb("one_hot", [P, NT, E])
        self.rank = sb("rank", [P, NT])
        self.here = sb("here", [P, E])


def build(nc, x, W_qkv, gate_w, sgw, suw, sdw, rgw, ruw, rdw, out):
    B, N, D = x.shape
    E, _, F = rgw.shape
    T = B * N
    NT, NG = T // P, T // GT
    ET = T // ST + E
    C = D // P
    x_g = x.rearrange("b n d -> (b n) d").rearrange("(g j p) d -> g p j d", p=P, j=GT // P)
    out_g = out.rearrange("b n d -> (b n) d").rearrange("(g j p) d -> g p j d", p=P, j=GT // P)
    xs = nc.dram_tensor("xs_rows", [T, D], F32).ap()
    sh = nc.dram_tensor("shared_rows", [T, D], F32).ap()
    dr = nc.dram_tensor("routed_rows", [ET * ST, D], F32).ap()
    xth = nc.dram_tensor("xT_high", [NG, P, C, GT], F32).ap()
    xtl = nc.dram_tensor("xT_low", [NG, P, C, GT], F32).ap()
    xs_g = xs.rearrange("(g j p) d -> g p j d", p=P, j=GT // P)
    sh_g = sh.rearrange("(g j p) d -> g p j d", p=P, j=GT // P)
    d_t = dr.rearrange("(t h p) d -> t p h d", p=P, h=ST // P)
    with ExitStack() as ctx:
        keep = Keep(nc, ctx, D, E, NT, (ET + 2) * ST // P, ET)
        with ExitStack() as early:
            ranks = Ranks(nc, early, E, NT)
            token_stage(nc, x_g, gate_w, sgw, suw, sdw, xs_g, xth, xtl, sh_g, keep, ranks, D, F, E, NG)
            routing_stage(nc, W_qkv, d_t, keep, ranks, D, E, NT, ET)
        expert_stage(nc, xs, rgw, ruw, rdw, d_t, keep, D, F, E, ET)
        attention_stage(nc, x_g, sh_g, dr, xth, xtl, out_g, keep, D, B, N)


_INS = ["L0_attn_x", "L0_attn_W_qkv", "L0_ffn_gate_w", "L0_ffn_shared_gate_w", "L0_ffn_shared_up_w",
        "L0_ffn_shared_down_w", "L0_ffn_routed_gate_w", "L0_ffn_routed_up_w", "L0_ffn_routed_down_w"]


def kernel(**inputs):
    import numpy as np
    from concourse import bacc
    from concourse.bass_utils import run_bass_kernel_spmd

    nc = bacc.Bacc("TRN2", target_bir_lowering=False, num_devices=1)
    arrays = {f"in_{n}": np.ascontiguousarray(inputs[n]) for n in _INS}
    args = [nc.dram_tensor(n, a.shape, mybir.dt.from_np(a.dtype), kind="ExternalInput").ap() for n, a in arrays.items()]
    out = nc.dram_tensor("out", inputs["L0_attn_x"].shape, F32, kind="ExternalOutput").ap()
    build(nc, *args, out)
    return run_bass_kernel_spmd(nc, [arrays], core_ids=[0]).results[0]["out"]
```

```python
from contextlib import ExitStack

import concourse.bass as bass
from concourse import mybir

F32 = mybir.dt.float32
F32R = mybir.dt.float32r
BF16 = mybir.dt.bfloat16
I32 = mybir.dt.int32
U32 = mybir.dt.uint32
ALU = mybir.AluOpType
ACT = mybir.ActivationFunctionType
AX = mybir.AxisListType

P = 128
EPS = 1e-5
EULER = 2.718281828459045
MASKED = -1e30
GT = 512
ST = 256


def wait(eng, sem, value):
    if isinstance(value, int) and value <= 0:
        return
    eng.wait_ge(sem, value)


def is_first(g):
    return isinstance(g, int) and g == 0


def wait_apart(eng, sem, value, passed):
    if isinstance(value, int) and value <= 0:
        return
    eng.wait_ge(sem, value)
    eng.sem_inc(passed, 1)


def each_pair(eng, n, body):
    for i in range(min(2, n - 1)):
        body(i, False)
    if n > 3:
        with eng.Fori(2, n - 1) as i:
            body(i, False)
    body(n - 1, True)


def split_matmuls(nc, out, hi, lo, rhi, rlo, first, last):
    nc.tensor.matmul(out, hi, rhi, start=first, stop=False, skip_group_check=True)
    nc.tensor.matmul(out, lo, rhi, start=False, stop=False, skip_group_check=True)
    return nc.tensor.matmul(out, hi, rlo, start=False, stop=last, skip_group_check=True)


def token_stage(nc, x_g, gate_w, sgw, suw, sdw, xs_g, xth_g, xtl_g, sh_g, keep, ranks, D, F, E, NG):
    C, J, IT = D // P, GT // P, F // P
    with ExitStack() as st:
        def sb(name, shape, dt=F32):
            return st.enter_context(nc.sbuf_tensor("a_" + name, shape, dt))

        def ps(name, shape):
            return st.enter_context(nc.psum_tensor("a_" + name, shape, F32))

        def sem(name):
            return st.enter_context(nc.semaphore("a_" + name))

        wraw = sb("wraw", [P, 3, IT * D])
        raw = [wraw[:, 0].rearrange("p (c f) -> p c f", c=C), wraw[:, 1].rearrange("p (c f) -> p c f", c=C),
               wraw[:, 2].rearrange("p (i d) -> p i d", i=IT)]
        w_hi = [sb("gw_hi", [P, C, F], F32R), sb("uw_hi", [P, C, F], F32R), sb("dw_hi", [P, IT, D], F32R)]
        w_lo = [sb("gw_lo", [P, C, F], F32R), sb("uw_lo", [P, C, F], F32R), sb("dw_lo", [P, IT, D], F32R)]
        maskf = sb("maskf", [P, P])
        expert_i = sb("expert_i", [P, E], I32)
        expert_f = sb("expert_f", [P, E])
        seen = sb("seen", [P, J + 1, E])
        mine = sb("mine", [P, J, E])
        gate = sb("gate", [P, C, E])
        gate_hl = sb("gate_hl", [P, C, 2, E], F32R)
        xt = sb("xt", [P, 2, J, D])
        stats = sb("stats", [P, 2, J, 6])
        mv = sb("mv", [P, 2, J, 2])
        ve = sb("ve", [P, 2, J])
        rstd = sb("rstd", [P, 2, J])
        xn = sb("xn", [P, 2, J, D])
        xT_hi = [sb(f"xT_hi{k}", [P, C, GT], F32R) for k in range(2)]
        xT_lo = [sb(f"xT_lo{k}", [P, C, GT], F32R) for k in range(2)]
        silu = sb("silu", [P, 2, GT])
        h32 = sb("h32", [P, IT, GT])
        h_hi = [sb(f"h_hi{k}", [P, IT, GT], F32R) for k in range(2)]
        h_lo = [sb(f"h_lo{k}", [P, IT, GT], F32R) for k in range(2)]
        sh = sb("sh", [P, 2, J, D])
        lgT = sb("lgT", [P, GT])
        lg2 = sb("lg2", [P, J, 2, E])
        lg = sb("lg", [P, J, E])
        top = sb("top", [P, J, 8])
        topi = sb("topi", [P, J, 8], U32)
        negtop = sb("negtop", [P, J])
        eneg = sb("eneg", [P, J])
        score = sb("score", [P, 2, J])
        xs = sb("xs", [P, 2, J, D])
        psT = ps("psT", [P, 2, 512])
        psG = ps("psG", [P, 2, 512])
        psU = ps("psU", [P, 2, 512])
        psD = ps("psD", [P, J, D])
        psLT = psT[0:2 * E, 0]
        psL = psT[:, 1].rearrange("p (j n) -> p j n", j=J)
        assert 2 * E <= P and GT == 512

        gate_in, w_hi_ok, w_ok, gate_ok = (sem(n) for n in ("gate_in", "w_hi_ok", "w_ok", "gate_ok"))
        w_in = [sem(f"w_in{n}") for n in range(3)]
        x_in = [sem(f"x_in{k}") for k in range(2)]
        xs_out = [sem(f"xs_out{k}") for k in range(2)]
        xt_out = [sem(f"xt_out{k}") for k in range(2)]
        sh_out = [sem(f"sh_out{k}") for k in range(2)]
        var_ok, rstd_ok, xn_ok, t_mm, xh_ok, xl_ok = (sem(n) for n in ("var_ok", "rstd_ok", "xn_ok", "t_mm", "xh_ok", "xl_ok"))
        g_mm, u_mm, silu_ok, h_ok, hhi_ok, hlo_ok, d_mm, sh_ok = (
            sem(n) for n in ("g_mm", "u_mm", "silu_ok", "h_ok", "hhi_ok", "hlo_ok", "d_mm", "sh_ok"))
        lgt_mm, lgt_ok, lg_mm, lg_ok, ntop_ok, eneg_ok, xs_ok, rt_step = (
            sem(n) for n in ("lgt_mm", "lgt_ok", "lg_mm", "lg_ok", "ntop_ok", "eneg_ok", "xs_ok", "rt_step"))
        rk_step, sg_step = sem("rk_step"), sem("sg_step")
        lgt_zero = sem("lgt_zero")
        ln_step, passed, zeroed, ident_ok, iota_ok = (sem(n) for n in ("ln_step", "passed", "zeroed", "ident_ok", "iota_ok"))
        block = st.enter_context(nc.Block())

        @block.sync
        def _(sp):
            sp.dma_start(xt[:, 0], x_g[0]).then_inc(x_in[0], 16)
            sp.dma_start(gate[:], gate_w.rearrange("(c p) e -> p c e", p=P)).then_inc(gate_in, 16)
            sp.dma_start(raw[0], sgw.rearrange("(c p) f -> p c f", p=P)).then_inc(w_in[0], 16)
            sp.dma_start(raw[1], suw.rearrange("(c p) f -> p c f", p=P)).then_inc(w_in[1], 16)
            sp.dma_start(raw[2], sdw.rearrange("(i p) d -> p i d", p=P)).then_inc(w_in[2], 16)
            sp.dma_start(xt[:, 1], x_g[1]).then_inc(x_in[1], 16)

            def store_xt(g, k):
                wait(sp, xh_ok, C * (g + 1))
                sp.dma_start(xth_g[g], xT_hi[k][:].bitcast(F32)).then_inc(xt_out[k], 16)
                wait(sp, xl_ok, C * (g + 1))
                sp.dma_start(xtl_g[g], xT_lo[k][:].bitcast(F32)).then_inc(xt_out[k], 16)

            def store_xs(g, k):
                wait(sp, xs_ok, g + 1)
                sp.dma_start(xs_g[g], xs[:, k]).then_inc(xs_out[k], 16)

            def store_sh(g, k):
                wait(sp, sh_ok, g + 1)
                sp.dma_start(sh_g[g], sh[:, k]).then_inc(sh_out[k], 16)

            store_xt(0, 0)

            def pair(i, last):
                for k in range(2):
                    g = 2 * i + k
                    if not last:
                        wait(sp, xn_ok, g + 1)
                        sp.dma_start(xt[:, k], x_g[g + 2]).then_inc(x_in[k], 16)
                    store_xs(g, k)
                    if not (last and k == 1):
                        store_xt(g + 1, 1 - k)
                    if not is_first(g):
                        store_sh(g - 1, 1 - k)
            each_pair(sp, NG // 2, pair)
            store_sh(NG - 1, 1)
            for k in range(2):
                sp.wait_ge(xt_out[k], 32 * (NG // 2))
                sp.wait_ge(xs_out[k], 16 * (NG // 2))
                sp.wait_ge(sh_out[k], 16 * (NG // 2))

        @block.gpsimd
        def _(pool):
            def rstd_of(g, k):
                wait(pool, var_ok, g + 1)
                nc.gpsimd.tensor_tensor(rstd[:, k], ve[:, k], keep.neghalf[:], ALU.pow).then_inc(rstd_ok, 1)

            def eneg_of(g):
                wait(pool, ntop_ok, g + 1)
                nc.gpsimd.tensor_tensor(eneg[:], keep.euler[:], negtop[:], ALU.pow).then_inc(eneg_ok, 1)

            g = nc.gpsimd
            g.memset(keep.neghalf[:], -0.5).then_inc(zeroed, 1)
            g.memset(keep.euler[:], EULER).then_inc(zeroed, 1)
            g.memset(keep.ident[:], 0.0).then_inc(zeroed, 1)
            g.memset(maskf[:], 0.0).then_inc(zeroed, 1)
            pool.wait_ge(zeroed, 4)
            g.affine_select(out=keep.ident[:], in_=keep.ident[:], compare_op=ALU.not_equal, fill=1.0,
                            base=0, pattern=[[-1, P]], channel_multiplier=1).then_inc(ident_ok, 1)
            g.iota(expert_i[:], pattern=[[1, E]], base=0, channel_multiplier=0).then_inc(iota_ok, 1)
            rstd_of(0, 0)
            g.affine_select(out=maskf[:], in_=maskf[:], compare_op=ALU.is_ge, fill=MASKED,
                            base=0, pattern=[[-1, P]], channel_multiplier=1).then_inc(ident_ok, 1)
            rstd_of(1, 1)

            def pair(i, last):
                for k in range(2):
                    g = 2 * i + k
                    eneg_of(g)
                    if not last:
                        rstd_of(g + 2, k)
            each_pair(pool, NG // 2, pair)

        @block.vector
        def _(dve):
            v = nc.vector
            v.memset(seen[:, 0], 0.0).then_inc(rt_step, 1)
            v.memset(lgT[:], 0.0).then_inc(lgt_zero, 1)
            dve.wait_ge(gate_in, 16)
            v.tensor_copy(gate_hl[:, :, 0], gate[:]).then_inc(gate_ok, 1)
            dve.wait_ge(gate_ok, 1)
            v.tensor_tensor(gate_hl[:, :, 1], gate[:], gate_hl[:, :, 0].bitcast(F32), ALU.subtract).then_inc(gate_ok, 1)

            def stats_of(g, k, i):
                wait(dve, x_in[k], 16 * (i + 1))
                for j in range(J):
                    s = v.bn_stats(stats[:, k, j], xt[:, k, j])
                s.then_inc(ln_step, 1)
                wait_apart(dve, ln_step, 2 * g + 1, passed)
                for j in range(J):
                    s = v.bn_aggr(mv[:, k, j], stats[:, k, j])
                s.then_inc(ln_step, 1)
                wait(dve, ln_step, 2 * g + 2)
                v.tensor_scalar(ve[:, k], mv[:, k, :, 1], EPS, None, ALU.add).then_inc(var_ok, 1)

            def norm(g, k):
                wait(dve, rstd_ok, g + 1)
                for j in range(J):
                    s = v.tensor_scalar(xn[:, k, j], xt[:, k, j], mv[:, k, j, 0:1], rstd[:, k, j:j + 1],
                                        ALU.subtract, ALU.mult)
                s.then_inc(xn_ok, 1)

            def xT_low(g, k, i):
                wait(dve, xt_out[k], 32 * i)
                for c in range(C):
                    wait(dve, xh_ok, C * g + c + 1)
                    v.tensor_tensor(xT_lo[k][:, c], psT[:, c], xT_hi[k][:, c].bitcast(F32), ALU.subtract).then_inc(xl_ok, 1)

            RS = J + 5

            def route(g):
                n = RS * g + 1
                wait(dve, lg_ok, g + 1)
                v.tensor_tensor(lg[:], lg2[:, :, 0], lg2[:, :, 1], ALU.add).then_inc(rt_step, 1)
                wait_apart(dve, rt_step, n + 1, passed)
                for j in range(J):
                    s = v.max(top[:, j], lg[:, j])
                s.then_inc(rt_step, 1)
                wait(dve, rt_step, n + 2)
                v.tensor_scalar(negtop[:], top[:, :, 0], -1.0, None, ALU.mult).then_inc(ntop_ok, 1)
                for j in range(J):
                    s = v.max_index(topi[:, j], top[:, j], lg[:, j])
                s.then_inc(rt_step, 1)

            def rank(g):
                n = RS * g + 4
                wait(dve, rt_step, n)
                for j in range(J):
                    s = v.tensor_scalar(ranks.one_hot[:, bass.ds(g * J + j, 1)].rearrange("p a e -> p (a e)"),
                                        expert_f[:], topi[:, j, 0:1], None, ALU.is_equal)
                s.then_inc(rt_step, 1)
                for j in range(J):
                    wait(dve, rt_step, n + 1 + j)
                    v.tensor_tensor(seen[:, j + 1], seen[:, j],
                                    ranks.one_hot[:, bass.ds(g * J + j, 1)].rearrange("p a e -> p (a e)"),
                                    ALU.add).then_inc(rt_step, 1)

            def rank_sum(g):
                n = RS * g + J + 5
                wait(dve, rt_step, n)
                v.tensor_tensor(mine[:], seen[:, 0:J], ranks.one_hot[:, bass.ds(g * J, J)], ALU.mult).then_inc(rk_step, 1)
                wait_apart(dve, rk_step, 2 * g + 2, passed)
                v.tensor_copy(seen[:, 0], seen[:, J]).then_inc(rt_step, 1)
                v.tensor_reduce(ranks.rank[:, bass.ds(g * J, J)], mine[:], AX.X, ALU.add).then_inc(rk_step, 1)

            def scale(g, k, i):
                wait(dve, eneg_ok, g + 1)
                v.tensor_scalar(eneg[:], eneg[:], 1.0, None, ALU.add).then_inc(sg_step, 1)
                wait(dve, sg_step, 2 * g + 1)
                v.reciprocal(score[:, k], eneg[:]).then_inc(sg_step, 1)
                wait(dve, sg_step, 2 * g + 2)
                wait(dve, xs_out[k], 16 * i)
                for j in range(J):
                    s = v.tensor_scalar(xs[:, k, j], xn[:, k, j], score[:, k, j:j + 1], None, ALU.mult)
                s.then_inc(xs_ok, 1)

            def mul(g, it):
                wait(dve, u_mm, IT * g + it + 1)
                wait(dve, silu_ok, IT * g + it + 1)
                wait(dve, hlo_ok, IT * (g - 1) + it + 1)
                v.tensor_tensor(h32[:, it], silu[:, it % 2], psU[:, it % 2], ALU.mult).then_inc(h_ok, 1)

            def h_low(g, k, it):
                wait(dve, hhi_ok, IT * g + it + 1)
                v.tensor_tensor(h_lo[k][:, it], h32[:, it], h_hi[k][:, it].bitcast(F32), ALU.subtract).then_inc(hlo_ok, 1)

            stats_of(0, 0, 0)
            norm(0, 0)
            for n in range(3):
                dve.wait_ge(w_hi_ok, n + 1)
                v.tensor_tensor(w_lo[n][:], raw[n], w_hi[n][:].bitcast(F32), ALU.subtract).then_inc(w_ok, 1)
                if n == 0:
                    xT_low(0, 0, 0)
            dve.wait_ge(iota_ok, 1)
            v.tensor_copy(expert_f[:], expert_i[:]).then_inc(rk_step, 1)
            dve.wait_ge(ident_ok, 2)
            v.tensor_copy(keep.ident_bf[:], keep.ident[:])
            v.tensor_copy(keep.mask_bf[:], maskf[:])
            stats_of(1, 1, 0)
            norm(1, 1)

            def pair(i, last):
                for k in range(2):
                    g = 2 * i + k
                    route(g)
                    mul(g, 0)
                    rank(g)
                    h_low(g, k, 0)
                    mul(g, 1)
                    scale(g, k, i)
                    h_low(g, k, 1)
                    if not (last and k == 1):
                        xT_low(g + 1, 1 - k, i + k)
                    mul(g, 2)
                    rank_sum(g)
                    h_low(g, k, 2)
                    mul(g, 3)
                    if not last:
                        stats_of(g + 2, k, i + 1)
                    h_low(g, k, 3)
                    if not last:
                        norm(g + 2, k)
            each_pair(dve, NG // 2, pair)
            dve.wait_ge(rt_step, 1 + RS * NG)
            v.tensor_copy(ranks.here[:], seen[:, 0])

        @block.scalar
        def _(act):
            s = nc.scalar

            def xT_high(g, k, i):
                wait(act, xt_out[k], 32 * i)
                wait(act, u_mm, IT * (g - 1))
                for c in range(C):
                    wait(act, t_mm, C * g + c + 1)
                    s.copy(xT_hi[k][:, c], psT[:, c]).then_inc(xh_ok, 1)

            def logits(g):
                wait(act, lg_mm, g + 1)
                s.copy(lg2[:].rearrange("p j a e -> p j (a e)"), psL[:, :, 0:2 * E]).then_inc(lg_ok, 1)

            def logits_T(g):
                wait(act, lgt_mm, g + 1)
                s.copy(lgT[0:2 * E], psLT).then_inc(lgt_ok, 1)

            def silu_of(g, it):
                wait(act, g_mm, IT * g + it + 1)
                wait(act, h_ok, IT * g + it - 1)
                s.activation(silu[:, it % 2], psG[:, it % 2], ACT.Silu).then_inc(silu_ok, 1)

            def h_high(g, k, it):
                wait(act, h_ok, IT * g + it + 1)
                wait(act, d_mm, g - 1)
                s.copy(h_hi[k][:, it], h32[:, it]).then_inc(hhi_ok, 1)

            def shared_out(g, k, i):
                wait(act, d_mm, g + 1)
                wait(act, sh_out[k], 16 * i)
                s.copy(sh[:, k], psD[:]).then_inc(sh_ok, 1)

            xT_high(0, 0, 0)
            for n in range(3):
                act.wait_ge(w_in[n], 16)
                s.copy(w_hi[n][:], raw[n]).then_inc(w_hi_ok, 1)
            act.wait_ge(lgt_zero, 1)
            logits_T(0)

            def pair(i, last):
                for k in range(2):
                    g = 2 * i + k
                    logits(g)
                    for it in range(IT):
                        silu_of(g, it)
                        h_high(g, k, it)
                        if it == 1 and not (last and k == 1):
                            xT_high(g + 1, 1 - k, i + k)
                    if not (last and k == 1):
                        logits_T(g + 1)
                    if not is_first(g):
                        shared_out(g - 1, 1 - k, i - 1 + k)
            each_pair(act, NG // 2, pair)
            shared_out(NG - 1, 1, NG // 2 - 1)

        @block.tensor
        def _(pe):
            def transposes(g, k):
                wait(pe, xn_ok, g + 1)
                wait(pe, lg_ok, g)
                wait(pe, xl_ok, C * g)
                for c in range(C):
                    for j in range(J):
                        mm = nc.tensor.transpose(psT[:, c, j * P:(j + 1) * P],
                                                 xn[:, k, j, c * P:(c + 1) * P], keep.ident[:])
                    mm.then_inc(t_mm, 1)

            def logits_T(g, k):
                wait(pe, xl_ok, C * (g + 1))
                for c in range(C):
                    nc.tensor.matmul(psLT, gate_hl[:, c].rearrange("p a e -> p (a e)"), xT_hi[k][:, c],
                                     start=(c == 0), stop=False, skip_group_check=True)
                for c in range(C):
                    mm = nc.tensor.matmul(psLT[0:E], gate_hl[:, c, 0], xT_lo[k][:, c],
                                          start=False, stop=(c == C - 1), skip_group_check=True)
                mm.then_inc(lgt_mm, 1)

            def logits(g):
                wait(pe, lgt_ok, g + 1)
                for j in range(J):
                    mm = nc.tensor.transpose(psL[:, j], lgT[:, j * P:(j + 1) * P], keep.ident[:])
                mm.then_inc(lg_mm, 1)

            def up(g, k, half):
                if half == 0:
                    wait(pe, xl_ok, C * (g + 1))
                if is_first(g):
                    pe.wait_ge(w_ok, 2)
                for it in range(half * IT // 2, (half + 1) * IT // 2):
                    cols = slice(it * P, (it + 1) * P)
                    wait(pe, silu_ok, IT * g + it - 1)
                    for c in range(C):
                        mm = split_matmuls(nc, psG[:, it % 2], w_hi[0][:, c, cols], w_lo[0][:, c, cols],
                                           xT_hi[k][:, c], xT_lo[k][:, c], c == 0, c == C - 1)
                    mm.then_inc(g_mm, 1)
                    wait(pe, h_ok, IT * g + it - 1)
                    for c in range(C):
                        mm = split_matmuls(nc, psU[:, it % 2], w_hi[1][:, c, cols], w_lo[1][:, c, cols],
                                           xT_hi[k][:, c], xT_lo[k][:, c], c == 0, c == C - 1)
                    mm.then_inc(u_mm, 1)

            def down(g, k, half):
                if is_first(g):
                    pe.wait_ge(w_ok, 3)
                if half == 0:
                    wait(pe, sh_ok, g)
                for it in range(half * IT // 2, (half + 1) * IT // 2):
                    wait(pe, hlo_ok, IT * g + it + 1)
                    for j in range(J):
                        cols = slice(j * P, (j + 1) * P)
                        mm = split_matmuls(nc, psD[:, j], h_hi[k][:, it, cols], h_lo[k][:, it, cols],
                                           w_hi[2][:, it], w_lo[2][:, it],
                                           it == 0 and j % 2 == 0, it == IT - 1)
                if half == 1:
                    mm.then_inc(d_mm, 1)

            pe.wait_ge(ident_ok, 1)
            transposes(0, 0)
            pe.wait_ge(gate_ok, 2)
            logits_T(0, 0)
            logits(0)

            def pair(i, last):
                for k in range(2):
                    g = 2 * i + k
                    up(g, k, 0)
                    if not (last and k == 1):
                        transposes(g + 1, 1 - k)
                    up(g, k, 1)
                    if not (last and k == 1):
                        logits_T(g + 1, 1 - k)
                    if not is_first(g):
                        down(g - 1, 1 - k, 0)
                    if not (last and k == 1):
                        logits(g + 1)
                    if not is_first(g):
                        down(g - 1, 1 - k, 1)
            each_pair(pe, NG // 2, pair)
            down(NG - 1, 1, 0)
            down(NG - 1, 1, 1)


def routing_stage(nc, W_qkv, d_t, keep, ranks, D, E, NT, ET):
    NC = keep.slot_token.shape[1]
    TT = keep.tile_expert.shape[1]
    C = D // P
    with ExitStack() as st:
        def sb(name, shape, dt=F32):
            return st.enter_context(nc.sbuf_tensor("r_" + name, shape, dt))

        def sem(name):
            return st.enter_context(nc.semaphore("r_" + name))

        nothing = sb("nothing", [P, ST // P, D])
        wqkv = sb("wqkv", [P, C, 3 * D])
        wT = sb("wT", [P, 2 * C, D])
        a32 = sb("a32", [P, C, D])
        zeros = sb("zeros", [P, E])
        counts = sb("counts", [P, 2, E])
        tiles_i = sb("tiles_i", [P, E], I32)
        tiles_s = sb("tiles_s", [P, E], I32)
        tiles = sb("tiles", [P, E])
        tiles_cum = sb("tiles_cum", [P, E])
        base = sb("base", [P, E])
        shift = sb("shift", [P, E])
        moved = sb("moved", [P, NT, E])
        start = sb("start", [P, NT])
        pos = sb("pos", [P, NT])
        pos_i = sb("pos_i", [P, NT], I32)
        lo_i = sb("lo_i", [P, NT], I32)
        hi_i = sb("hi_i", [P, NT], I32)
        lo = sb("lo", [P, NT])
        hi = sb("hi", [P, NT])
        col_i = sb("col_i", [P, max(NC, P)], I32)
        token_i = sb("token_i", [P, NT], I32)
        col = sb("col", [P, max(NC, P)])
        token = sb("token", [P, NT])
        below = sb("below", [P, P])
        ones = sb("ones", [P, P])
        away = sb("away", [P, 2, P])
        neglo = sb("neglo", [P, NT])
        lo_hot = sb("lo_hot", [P, 4, P])
        hi_hot = sb("hi_hot", [P, 4, NC])
        past = sb("past", [P, E])
        tile_f = sb("tile_f", [P, 1])
        used = sb("used", [1, 1], I32)
        psC = st.enter_context(nc.psum_tensor("r_psC", [P, 2, E], F32))
        psS = st.enter_context(nc.psum_tensor("r_psS", [P, 512], F32))
        psE = st.enter_context(nc.psum_tensor("r_psE", [P, P], F32))
        psT = st.enter_context(nc.psum_tensor("r_psT", [P, 2 * C, D], F32))
        psA = st.enter_context(nc.psum_tensor("r_psA", [P, C, 2 * D], F32))
        zero_ok, zero_out, te_ok, te_mm = (sem(n) for n in ("zero_ok", "zero_out", "te_ok", "te_mm"))
        lo_ok, away_ok, odd_ok = (sem(n) for n in ("lo_ok", "away_ok", "odd_ok"))
        assert TT <= P and NT % 4 == 0
        consts, c_mm, step, hot_ok, s_mm, w_in, wt_mm, wt_ok, a_mm, a_ok, split_ok = (
            sem(n) for n in ("consts", "c_mm", "step", "hot_ok", "s_mm", "w_in",
                             "wt_mm", "wt_ok", "a_mm", "a_ok", "split_ok"))
        block = st.enter_context(nc.Block())

        @block.sync
        def _(sp):
            sp.dma_start(wqkv[:], W_qkv.rearrange("(c p) n -> p c n", p=P)).then_inc(w_in, 16)
            sp.wait_ge(zero_ok, 1)
            with sp.Fori(NT * P // ST, ET) as t:
                sp.dma_start(d_t[t], nothing[:]).then_inc(zero_out, 16)
            sp.wait_ge(zero_out, 16 * (ET - NT * P // ST))

        @block.gpsimd
        def _(pool):
            g = nc.gpsimd
            g.memset(nothing[:], 0.0).then_inc(zero_ok, 1)
            g.memset(ones[:], 1.0).then_inc(consts, 1)
            pool.wait_ge(consts, 1)
            g.affine_select(out=below[:], in_=ones[:], compare_op=ALU.is_gt, fill=0.0,
                            base=0, pattern=[[1, P]], channel_multiplier=-1).then_inc(consts, 1)
            g.iota(col_i[:], pattern=[[1, col_i.shape[1]]], base=0, channel_multiplier=0).then_inc(consts, 1)
            g.iota(token_i[:], pattern=[[P, NT]], base=0, channel_multiplier=1).then_inc(consts, 1)
            pool.wait_ge(split_ok, 1)
            g.tensor_tensor(keep.v_lo[:], wqkv[:, :, 2 * D:3 * D], keep.v_hi[:].bitcast(F32), ALU.subtract)
            pool.wait_ge(split_ok, 2)
            g.tensor_tensor(keep.a_lo[:], a32[:], keep.a_hi[:].bitcast(F32), ALU.subtract)

        @block.scalar
        def _(act):
            s = nc.scalar
            act.wait_ge(w_in, 16)
            s.copy(keep.v_hi[:], wqkv[:, :, 2 * D:3 * D]).then_inc(split_ok, 1)
            act.wait_ge(wt_mm, 1)
            s.copy(wT[:], psT[:]).then_inc(wt_ok, 1)
            act.wait_ge(a_mm, 1)
            s.mul(a32[:], psA[:, :, 0:D], float(D) ** -0.5).then_inc(a_ok, 1)
            act.wait_ge(a_ok, 1)
            s.copy(keep.a_hi[:], a32[:]).then_inc(split_ok, 1)
            act.wait_ge(lo_ok, 1)

            def spread(i, last):
                for k in range(2):
                    t = 4 * i + 2 * k + 1
                    wait(act, odd_ok, 2 * i + k - 1)
                    s.activation(away[:, k], col[:, 0:P], ACT.Abs, bias=neglo[:, bass.ds(t, 1)]).then_inc(away_ok, 1)
                for k in range(2):
                    wait(act, away_ok, 2 * i + k + 1)
                    wait(act, s_mm, 4 * i + 2 * k - 2)
                    s.activation(lo_hot[:, 2 * k + 1], away[:, k], ACT.Relu, bias=1.0, scale=-1.0).then_inc(odd_ok, 1)
            each_pair(act, NT // 4, spread)

        @block.vector
        def _(dve):
            v = nc.vector
            n = [0]

            def done(ins):
                n[0] += 1
                ins.then_inc(step, 1)
                dve.wait_ge(step, n[0])

            v.memset(zeros[:], 0.0)
            dve.wait_ge(c_mm, 1)
            done(v.tensor_copy(counts[:], psC[:]))
            done(v.tensor_scalar(tiles_i[:], counts[:, 1], float(ST - 1), None, ALU.add))
            done(v.tensor_scalar(tiles_s[:], tiles_i[:], ST.bit_length() - 1, None, ALU.arith_shift_right))
            done(v.tensor_copy(tiles[:], tiles_s[:]))
            done(v.tensor_tensor_scan(tiles_cum[:], zeros[:], tiles[:], 0.0, ALU.add, ALU.add))
            done(v.tensor_tensor(base[:], tiles_cum[:], tiles[:], ALU.subtract))
            done(v.scalar_tensor_tensor(out=shift[:], in0=base[:], scalar=float(ST), in1=counts[:, 0],
                                        op0=ALU.mult, op1=ALU.add))
            done(v.tensor_tensor(moved[:], ranks.one_hot[:], shift[:].unsqueeze(1).to_broadcast([P, NT, E]), ALU.mult))
            done(v.tensor_reduce(start[:], moved[:], AX.X, ALU.add))
            done(v.tensor_tensor(pos[:], start[:], ranks.rank[:], ALU.add))
            done(v.tensor_copy(pos_i[:], pos[:]))
            v.tensor_scalar(hi_i[:], pos_i[:], P.bit_length() - 1, None, ALU.arith_shift_right)
            done(v.tensor_scalar(lo_i[:], pos_i[:], P - 1, None, ALU.bitwise_and))
            dve.wait_ge(consts, 4)
            v.tensor_copy(col[:], col_i[:])
            v.tensor_copy(token[:], token_i[:])
            v.tensor_copy(hi[:], hi_i[:])
            done(v.tensor_copy(lo[:], lo_i[:]))
            v.tensor_scalar(neglo[:], lo[:], -1.0, None, ALU.mult).then_inc(lo_ok, 1)
            done(v.tensor_scalar(past[:], tiles_cum[:], token[:, 0:1], None, ALU.is_le))
            done(v.tensor_reduce(tile_f[:], past[:], AX.X, ALU.add))
            v.tensor_scalar(tile_f[:], tile_f[:], float(E - 1), None, ALU.min).then_inc(te_ok, 1)

            def spread(i, last):
                for k in range(4):
                    t = 4 * i + k
                    wait(dve, s_mm, t - 3)
                    if k % 2 == 0:
                        v.tensor_scalar(lo_hot[:, k], col[:, 0:P], lo[:, bass.ds(t, 1)], None, ALU.is_equal)
                    v.tensor_scalar(hi_hot[:, k], col[:, 0:NC], hi[:, bass.ds(t, 1)], token[:, bass.ds(t, 1)],
                                    ALU.is_equal, ALU.mult).then_inc(hot_ok, 1)
            each_pair(dve, NT // 4, spread)

            v.tensor_copy(keep.position[:], pos_i[:])
            dve.wait_ge(te_mm, 1)
            v.tensor_copy(keep.tile_expert[:], psE[0:1, 0:TT])
            done(v.tensor_scalar(used[:], tiles_cum[0:1, E - 1:E], -1.0, None, ALU.add))
            v.tensor_scalar(keep.last_pair[:], used[:], 1, None, ALU.arith_shift_right)
            dve.wait_ge(s_mm, NT)
            v.tensor_copy(keep.slot_token[:], psS[:, 0:NC])

        @block.tensor
        def _(pe):
            pe.wait_ge(consts, 2)
            nc.tensor.matmul(psC[:, 0], below[:], ranks.here[:], start=True, stop=True)
            nc.tensor.matmul(psC[:, 1], ones[:], ranks.here[:], start=True, stop=True).then_inc(c_mm, 1)
            pe.wait_ge(w_in, 16)
            for w in range(2):
                for e in range(C):
                    for c in range(C):
                        mm = nc.tensor.transpose(psT[:, w * C + e, c * P:(c + 1) * P],
                                                 wqkv[:, c, w * D + e * P:w * D + (e + 1) * P], keep.ident[:])
            mm.then_inc(wt_mm, 1)
            pe.wait_ge(wt_ok, 1)
            for c in range(C):
                for e in range(C):
                    mm = nc.tensor.matmul(psA[:, c, 0:D], wT[:, e, c * P:(c + 1) * P], wT[:, C + e, :],
                                          start=(e == 0), stop=(e == C - 1))
            mm.then_inc(a_mm, 1)

            pe.wait_ge(te_ok, 1)
            nc.tensor.transpose(psE[0:1, :], tile_f[:], keep.ident[:]).then_inc(te_mm, 1)

            def gather(i, last):
                for k in range(4):
                    t = 4 * i + k
                    wait(pe, hot_ok, t + 1)
                    if k % 2 == 1:
                        wait(pe, odd_ok, 2 * i + k // 2 + 1)
                    nc.tensor.matmul(psS[:, 0:NC], lo_hot[:, k], hi_hot[:, k], start=is_first(t),
                                     stop=(last and k == 3), skip_group_check=True).then_inc(s_mm, 1)
            each_pair(pe, NT // 4, gather)


def expert_stage(nc, xs, rgw, ruw, rdw, d_t, keep, D, F, E, ET):
    C, H, IT = D // P, ST // P, F // P
    Q = IT // 2
    with ExitStack() as st:
        def sb(name, shape, dt=F32):
            return st.enter_context(nc.sbuf_tensor("e_" + name, shape, dt))

        def ps(name, shape):
            return st.enter_context(nc.psum_tensor("e_" + name, shape, F32))

        def sem(name):
            return st.enter_context(nc.semaphore("e_" + name))

        raw = [sb(f"raw{k}", [P, 3, C * F]) for k in range(2)]
        whi = [sb(f"whi{k}", [P, 3, C * F], F32R) for k in range(2)]
        wlo = [sb(f"wlo{k}", [P, 3, C * F], F32R) for k in range(2)]
        slot = sb("slot", [P, 2, H], I32)
        xg = sb("xg", [P, 2, H, D])
        x_hi = sb("x_hi", [P, 2, C, ST], F32R)
        x_lo = sb("x_lo", [P, 2, C, ST], F32R)
        silu = sb("silu", [P, 2, 2 * ST])
        h32 = sb("h32", [P, 2, 2 * ST])
        h_hi = [sb(f"h_hi{k}", [P, Q, 2 * ST], F32R) for k in range(2)]
        h_lo = [sb(f"h_lo{k}", [P, Q, 2 * ST], F32R) for k in range(2)]
        dout = sb("dout", [P, 2, H, D])
        psT = ps("psT", [P, C, ST])
        psG = ps("psG", [P, 2, 2, ST])
        psU = ps("psU", [P, 2, 2, ST])
        psD = ps("psD", [P, H, D])
        w_in = [sem(f"w_in{k}") for k in range(2)]
        x_in = [sem(f"x_in{k}") for k in range(2)]
        d_out = [sem(f"d_out{k}") for k in range(2)]
        passed = sem("passed")
        slot_ok, t_mm, xh_ok, xl_ok = (sem(n) for n in ("slot_ok", "t_mm", "xh_ok", "xl_ok"))
        wd_in = [sem(f"wd_in{k}") for k in range(2)]
        whi_ok, wlo_ok = sem("whi_ok"), sem("wlo_ok")
        wdh_ok, wdl_ok = sem("wdh_ok"), sem("wdl_ok")
        g_mm, u_mm, silu_ok, h_ok, hhi_ok, hlo_ok, d_mm, do_ok = (
            sem(n) for n in ("g_mm", "u_mm", "silu_ok", "h_ok", "hhi_ok", "hlo_ok", "d_mm", "do_ok"))
        block = st.enter_context(nc.Block())

        def part(w, k, n):
            v = w[k][:, n]
            return v.rearrange("p (c f) -> p c f", c=C) if n < 2 else v.rearrange("p (i d) -> p i d", i=IT)

        def tiles(eng, body):
            R = eng.value_load(keep.last_pair[0:1, 0:1], min_val=1, max_val=ET // 2 - 1)
            for i in range(2):
                for k in range(2):
                    body(2 * i + k, k, i)
            with eng.Fori(2, ET // 2) as i:
                with eng.If(i < R + 1):
                    for k in range(2):
                        body(2 * i + k, k, i)
            return R

        @block.sync
        def _(sp):
            def expert_of(t):
                return sp.value_load(keep.tile_expert[0:1, bass.ds(t, 1)], min_val=0, max_val=E - 1)

            def load_up(t, k):
                wait_apart(sp, wlo_ok, 2 * (t - 1), passed)
                e = expert_of(t)
                sp.dma_start(part(raw, k, 0), rgw[e].rearrange("(c p) f -> p c f", p=P)).then_inc(w_in[k], 16)
                sp.dma_start(part(raw, k, 1), ruw[e].rearrange("(c p) f -> p c f", p=P)).then_inc(w_in[k], 16)

            def load_down(t, k):
                wait_apart(sp, wdl_ok, t - 1, passed)
                e = expert_of(t)
                sp.dma_start(part(raw, k, 2), rdw[e].rearrange("(i p) d -> p i d", p=P)).then_inc(wd_in[k], 16)

            def store(t, k):
                wait(sp, do_ok, t + 1)
                sp.dma_start(d_t[t], dout[:, k]).then_inc(d_out[k], 16)

            for t in range(2):
                load_up(t, t)
                load_down(t, t)
            load_up(2, 0)

            def step(t, k, i):
                load_up(t + 3, 1 - k)
                load_down(t + 2, k)
                if not is_first(t):
                    store(t - 1, 1 - k)
            R = tiles(sp, step)
            store(R * 2 + 1, 1)
            for k in range(2):
                wait_apart(sp, w_in[k], (R + (3 - k)) * 32, passed)
                wait_apart(sp, wd_in[k], (R + 2) * 16, passed)
                wait_apart(sp, d_out[k], (R + 1) * 16, passed)

        @block.gpsimd
        def _(pool):
            g = nc.gpsimd

            def gather(t, k, i):
                wait_apart(pool, x_in[k], 16 * H * i, passed)
                g.tensor_copy(slot[:, k], keep.slot_token[:, bass.ds(t * H, H)]).then_inc(slot_ok, 1)
                wait(pool, t_mm, t - 1)
                wait_apart(pool, slot_ok, t + 1, passed)
                for h in range(H):
                    g.indirect_dma_start(out=xg[:, k, h], out_offset=None, in_=xs,
                                         in_offset=bass.IndirectOffsetOnAxis(slot[:, k, h:h + 1], 0)).then_inc(x_in[k], 16)

            def high_down(t, k, i):
                wait(pool, d_mm, t - 1)
                wait_apart(pool, wd_in[k], 16 * (i + 1), passed)
                g.tensor_copy(whi[k][:, 2], raw[k][:, 2]).then_inc(wdh_ok, 1)

            gather(0, 0, 0)
            gather(1, 1, 0)

            def step(t, k, i):
                high_down(t, k, i)
                gather(t + 2, k, i + 1)
            R = tiles(pool, step)
            for k in range(2):
                wait_apart(pool, x_in[k], (R + 2) * (16 * H), passed)

        @block.vector
        def _(dve):
            v = nc.vector

            def low(t, k, n):
                wait(dve, whi_ok, 2 * t + n + 1)
                v.tensor_tensor(wlo[k][:, n], raw[k][:, n], whi[k][:, n].bitcast(F32), ALU.subtract).then_inc(wlo_ok, 1)

            def low_down(t, k):
                wait(dve, wdh_ok, t + 1)
                v.tensor_tensor(wlo[k][:, 2], raw[k][:, 2], whi[k][:, 2].bitcast(F32), ALU.subtract).then_inc(wdl_ok, 1)

            def x_low(t, k):
                wait(dve, xh_ok, t + 1)
                v.tensor_tensor(x_lo[:, k], psT[:], x_hi[:, k].bitcast(F32), ALU.subtract).then_inc(xl_ok, 1)

            def mul(t, q):
                wait(dve, u_mm, Q * t + q + 1)
                wait(dve, silu_ok, Q * t + q + 1)
                wait(dve, hlo_ok, Q * (t - 1) + q + 1)
                v.tensor_tensor(h32[:, q], silu[:, q], psU[:, q].rearrange("p a n -> p (a n)"), ALU.mult).then_inc(h_ok, 1)

            def h_low(t, k, q):
                wait(dve, hhi_ok, Q * t + q + 1)
                v.tensor_tensor(h_lo[k][:, q], h32[:, q], h_hi[k][:, q].bitcast(F32), ALU.subtract).then_inc(hlo_ok, 1)

            low(0, 0, 0)
            x_low(0, 0)
            low(0, 0, 1)

            def step(t, k, i):
                low(t + 1, 1 - k, 0)
                mul(t, 0)
                low(t + 1, 1 - k, 1)
                h_low(t, k, 0)
                mul(t, 1)
                low_down(t, k)
                x_low(t + 1, 1 - k)
                h_low(t, k, 1)
            tiles(dve, step)

        @block.scalar
        def _(act):
            s = nc.scalar

            def high(t, k, i, n):
                if n == 0:
                    wait(act, w_in[k], 32 * (i + 1))
                    wait(act, u_mm, Q * (t - 1))
                s.copy(whi[k][:, n], raw[k][:, n]).then_inc(whi_ok, 1)

            def x_high(t, k):
                wait(act, t_mm, t + 1)
                s.copy(x_hi[:, k], psT[:]).then_inc(xh_ok, 1)

            def silu_of(t, q):
                wait(act, g_mm, Q * t + q + 1)
                wait(act, h_ok, Q * (t - 1) + q + 1)
                s.activation(silu[:, q], psG[:, q].rearrange("p a n -> p (a n)"), ACT.Silu).then_inc(silu_ok, 1)

            def h_high(t, k, q):
                wait(act, h_ok, Q * t + q + 1)
                s.copy(h_hi[k][:, q], h32[:, q]).then_inc(hhi_ok, 1)

            def d_copy(t, k, i):
                wait(act, d_mm, t + 1)
                wait(act, d_out[k], 16 * i)
                s.copy(dout[:, k], psD[:]).then_inc(do_ok, 1)

            high(0, 0, 0, 0)
            x_high(0, 0)
            high(0, 0, 0, 1)

            def step(t, k, i):
                high(t + 1, 1 - k, i + k, 0)
                silu_of(t, 0)
                high(t + 1, 1 - k, i + k, 1)
                h_high(t, k, 0)
                silu_of(t, 1)
                h_high(t, k, 1)
                x_high(t + 1, 1 - k)
                if not is_first(t):
                    d_copy(t - 1, 1 - k, i - 1 + k)
            R = tiles(act, step)
            d_copy(R * 2 + 1, 1, R)

        @block.tensor
        def _(pe):
            def transposes(t, k, i):
                wait(pe, x_in[k], 16 * H * (i + 1))
                wait(pe, xl_ok, t)
                for c in range(C):
                    for h in range(H):
                        mm = nc.tensor.transpose(psT[:, c, h * P:(h + 1) * P], xg[:, k, h, c * P:(c + 1) * P], keep.ident[:])
                mm.then_inc(t_mm, 1)

            def up(t, k):
                wait(pe, xl_ok, t + 1)
                for q in range(Q):
                    for n, (psum, freed, out) in enumerate(((psG, silu_ok, g_mm), (psU, h_ok, u_mm))):
                        wait(pe, wlo_ok, 2 * t + n + 1)
                        wait(pe, freed, Q * (t - 1) + q + 1)
                        for a in range(2):
                            cols = slice((2 * q + a) * P, (2 * q + a + 1) * P)
                            for c in range(C):
                                mm = split_matmuls(nc, psum[:, q, a], part(whi, k, n)[:, c, cols], part(wlo, k, n)[:, c, cols],
                                                   x_hi[:, k, c], x_lo[:, k, c], c == 0, c == C - 1)
                        mm.then_inc(out, 1)

            def down(t, k):
                wait(pe, wdl_ok, t + 1)
                wait(pe, do_ok, t)
                for it in range(IT):
                    wait(pe, hlo_ok, Q * t + it // 2 + 1)
                    for h in range(H):
                        cols = slice((it % 2) * ST + h * P, (it % 2) * ST + (h + 1) * P)
                        mm = split_matmuls(nc, psD[:, h], h_hi[k][:, it // 2, cols], h_lo[k][:, it // 2, cols],
                                           part(whi, k, 2)[:, it], part(wlo, k, 2)[:, it],
                                           it == 0 and h == 0, it == IT - 1)
                mm.then_inc(d_mm, 1)

            transposes(0, 0, 0)

            def step(t, k, i):
                up(t, k)
                transposes(t + 1, 1 - k, i + k)
                if not is_first(t):
                    down(t - 1, 1 - k)
            R = tiles(pe, step)
            down(R * 2 + 1, 1)


def attention_stage(nc, x_g, sh_g, d_rows, xth_g, xtl_g, out_g, keep, D, B, N):
    C, NB, GB = D // P, N // P, N // GT
    J = GT // P
    QU = C * GB
    VU = NB // 2
    groups = [i // 4 + 1 for i in range(NB)]
    before = [sum(groups[:i]) for i in range(NB + 1)]
    TG = before[NB]
    assert TG % 4 == 0 and NB % 2 == 0 and C * GB % 4 == 0
    with ExitStack() as st:
        def sb(name, shape, dt=F32):
            return st.enter_context(nc.sbuf_tensor("t_" + name, shape, dt))

        def ps(name, shape):
            return st.enter_context(nc.psum_tensor("t_" + name, shape, F32))

        def sem(name):
            return st.enter_context(nc.semaphore("t_" + name))

        x_hi = [sb(f"x_hi{k}", [P, C, N], F32R) for k in range(2)]
        x_lo = [sb(f"x_lo{k}", [P, C, N], F32R) for k in range(2)]
        q_hi = sb("q_hi", [P, C, N], F32R)
        q_lo = sb("q_lo", [P, C, N], F32R)
        v_hi = sb("v_hi", [P, NB, D], F32R)
        v_lo = sb("v_lo", [P, NB, D], F32R)
        prob = [sb(f"prob{k}", [P, N]) for k in range(2)]
        pT_hi = [sb(f"pT_hi{k}", [P, 4, P], F32R) for k in range(4)]
        pT_lo = [sb(f"pT_lo{k}", [P, 4, P], F32R) for k in range(4)]
        xr = sb("xr", [P, 2, J, D])
        shr = sb("shr", [P, 2, J, D])
        pos = sb("pos", [P, 2, 1], I32)
        routed = sb("routed", [P, 2, D])
        sum1 = sb("sum1", [P, 2, D])
        base = sb("base", [P, 2, D])
        negmax = sb("negmax", [P, 2])
        rowsum = sb("rowsum", [P, 2])
        rinv = sb("rinv", [P, 2])
        outb = sb("outb", [P, 2, D])
        psS = ps("psS", [P, 4, 512])
        psT = ps("psT", [P, 3, 4, P])
        psO = ps("psO", [P, 2, D])
        x_in = [[sem(f"x_in{k}_{g}") for g in range(GB)] for k in range(2)]
        r_in = [sem(f"r_in{k}") for k in range(2)]
        d_in = [sem(f"d_in{k}") for k in range(2)]
        o_out = [sem(f"o_out{k}") for k in range(2)]
        q_mm, qh_ok, ql_ok, v_mm, vh_ok, vl_ok = (sem(n) for n in ("q_mm", "qh_ok", "ql_ok", "v_mm", "vh_ok", "vl_ok"))
        s_mm, max_ok, exp_ok, t_mm, ph_ok, pl_ok, pv_mm, o_ok, rinv_ok = (
            sem(n) for n in ("s_mm", "max_ok", "exp_ok", "t_mm", "ph_ok", "pl_ok", "pv_mm", "o_ok", "rinv_ok"))
        passed = sem("passed")
        pos_ok, sum_ok, base_ok = (sem(n) for n in ("pos_ok", "sum_ok", "base_ok"))
        block = st.enter_context(nc.Block())

        def width(i):
            n = (i + 1) * P
            return [max(256, min(512, n - c)) for c in range(0, n, 512)]

        @block.sync
        def _(sp):
            def load_xt(b, k, u):
                g, low = u // 2, u % 2
                x, xt_g = (x_lo, xtl_g) if low else (x_hi, xth_g)
                sp.dma_start(x[k][:, :, g * GT:(g + 1) * GT].bitcast(F32), xt_g[b * GB + g]).then_inc(x_in[k][g], 16)

            def load_rows(n, k):
                wait(sp, base_ok, J * (n - 1))
                sp.dma_start(xr[:, k], x_g[n]).then_inc(r_in[k], 16)
                sp.dma_start(shr[:, k], sh_g[n]).then_inc(r_in[k], 16)

            for u in range(2 * GB):
                load_xt(0, 0, u)
            load_rows(0, 0)
            load_rows(1, 1)

            def pair(i, last):
                for k in range(2):
                    b = 2 * i + k
                    for g in range(GB):
                        for j in range(J):
                            r = b * NB + g * J + j
                            wait(sp, o_ok, r + 1)
                            sp.dma_start(out_g[b * GB + g][:, j], outb[:, j % 2]).then_inc(o_out[j % 2], 16)
                            u = g * J + j - (NB - 2 * GB - 2)
                            if 0 <= u < 2 * GB and not (last and k == 1):
                                if u == 0:
                                    wait(sp, s_mm, NB * b)
                                load_xt(b + 1, 1 - k, u)
                        if not (last and k == 1 and g >= GB - 2):
                            load_rows(b * GB + g + 2, g % 2)
            each_pair(sp, B // 2, pair)
            for k in range(2):
                sp.wait_ge(o_out[k], 16 * (B * NB // 2))

        @block.gpsimd
        def _(pool):
            g = nc.gpsimd

            def gather(r, k, n):
                wait(pool, sum_ok, r - 1)
                wait_apart(pool, d_in[k], 16 * n, passed)
                g.tensor_copy(pos[:, k], keep.position[:, bass.ds(r, 1)]).then_inc(pos_ok, 1)
                wait_apart(pool, pos_ok, r + 1, passed)
                g.indirect_dma_start(out=routed[:, k], out_offset=None, in_=d_rows,
                                     in_offset=bass.IndirectOffsetOnAxis(pos[:, k, 0:1], 0)).then_inc(d_in[k], 16)

            gather(0, 0, 0)
            gather(1, 1, 0)

            def pair(i, last):
                for t in range(2 * NB):
                    r = i * 2 * NB + t
                    k, kg, j = t % 2, (t // J) % 2, t % J
                    if j == 0:
                        wait(pool, r_in[kg], 32 * (i * GB + t // (2 * J) + 1))
                    wait(pool, d_in[k], 16 * (i * NB + t // 2 + 1))
                    wait(pool, o_ok, r - 1)
                    g.tensor_tensor(sum1[:, k], routed[:, k], shr[:, kg, j], ALU.add).then_inc(sum_ok, 1)
                    wait(pool, sum_ok, r + 1)
                    g.tensor_tensor(base[:, k], sum1[:, k], xr[:, kg, j], ALU.add).then_inc(base_ok, 1)
                    if not (last and t >= 2 * NB - 2):
                        gather(r + 2, k, i * NB + t // 2 + 1)
            each_pair(pool, B // 2, pair)

        @block.vector
        def _(dve):
            v = nc.vector

            def q_low(b, u):
                wait(dve, qh_ok, QU * b + u + 1)
                c, n = u % C, u // C
                v.tensor_tensor(q_lo[:, c, n * 512:(n + 1) * 512], psS[:, u % 4],
                                q_hi[:, c, n * 512:(n + 1) * 512].bitcast(F32), ALU.subtract).then_inc(ql_ok, 1)

            def v_low(b, u):
                wait(dve, vh_ok, VU * b + u + 1)
                v.tensor_tensor(v_lo[:, 2 * u:2 * u + 2].rearrange("p a d -> p (a d)"), psS[:, 2 + u % 2],
                                v_hi[:, 2 * u:2 * u + 2].rearrange("p a d -> p (a d)").bitcast(F32),
                                ALU.subtract).then_inc(vl_ok, 1)

            def row_max(b, i):
                r = b * NB + i
                wait(dve, s_mm, r + 1)
                wait(dve, exp_ok, r - 1)
                v.tensor_reduce(negmax[:, i % 2:i % 2 + 1], psS[:].rearrange("p a n -> p (a n)")[:, 0:(i + 1) * P],
                                AX.X, ALU.max, negate=True).then_inc(max_ok, 1)

            def p_low(b, i, q):
                n = b * TG + before[i] + q
                s = (before[i] + q) % 4
                m = min(4, i + 1 - 4 * q)
                wait(dve, ph_ok, n + 1)
                v.tensor_tensor(pT_lo[s][:, 0:m], psT[:, (before[i] + q) % 3, 0:m], pT_hi[s][:, 0:m].bitcast(F32),
                                ALU.subtract).then_inc(pl_ok, 1)

            def output(b, i, half):
                r = b * NB + i
                k = i % 2
                v.reciprocal(rinv[:, k:k + 1], rowsum[:, k:k + 1]).then_inc(rinv_ok, 1)
                wait(dve, rinv_ok, r + 1)
                wait(dve, pv_mm, b * TG + before[i + 1])
                wait(dve, base_ok, r + 1)
                wait(dve, o_out[k], 16 * half)
                v.scalar_tensor_tensor(out=outb[:, k], in0=psO[:, k], scalar=rinv[:, k:k + 1], in1=base[:, k],
                                       op0=ALU.mult, op1=ALU.add).then_inc(o_ok, 1)

            for u in range(QU):
                q_low(0, u)

            def pair(p, last):
                for k in range(2):
                    b = 2 * p + k
                    v_low(b, 0)
                    row_max(b, 0)
                    v_low(b, 1)
                    for i in range(NB):
                        for q in range(min(3, groups[i])):
                            p_low(b, i, q)
                        if i + 1 < NB:
                            row_max(b, i + 1)
                            if i + 2 < VU:
                                v_low(b, i + 2)
                        elif not (last and k == 1):
                            for u in range(QU // 2):
                                q_low(b + 1, u)
                        for q in range(3, groups[i]):
                            p_low(b, i, q)
                        if i + 1 == NB and not (last and k == 1):
                            for u in range(QU // 2, QU):
                                q_low(b + 1, u)
                        output(b, i, b * (NB // 2) + i // 2)
            each_pair(dve, B // 2, pair)

        @block.scalar
        def _(act):
            s = nc.scalar

            def q_high(b, u):
                c, n = u % C, u // C
                wait(act, q_mm, QU * b + u + 1)
                s.copy(q_hi[:, c, n * 512:(n + 1) * 512], psS[:, u % 4]).then_inc(qh_ok, 1)

            def v_high(b, u):
                wait(act, v_mm, VU * b + u + 1)
                s.copy(v_hi[:, 2 * u:2 * u + 2].rearrange("p a d -> p (a d)"), psS[:, 2 + u % 2]).then_inc(vh_ok, 1)

            def exp(b, i):
                r = b * NB + i
                wait(act, max_ok, r + 1)
                wait(act, o_ok, r - 1)
                s.activation(prob[i % 2][:, 0:(i + 1) * P], psS[:].rearrange("p a n -> p (a n)")[:, 0:(i + 1) * P],
                             ACT.Exp, bias=negmax[:, i % 2:i % 2 + 1], accum_out=rowsum[:, i % 2:i % 2 + 1]).then_inc(exp_ok, 1)

            def p_high(b, i, q):
                n = b * TG + before[i] + q
                t = (before[i] + q) % 4
                m = min(4, i + 1 - 4 * q)
                wait(act, t_mm, n + 1)
                wait(act, pv_mm, n - 3)
                s.copy(pT_hi[t][:, 0:m], psT[:, (before[i] + q) % 3, 0:m]).then_inc(ph_ok, 1)

            for u in range(QU):
                q_high(0, u)

            def pair(p, last):
                for k in range(2):
                    b = 2 * p + k
                    v_high(b, 0)
                    exp(b, 0)
                    v_high(b, 1)
                    for i in range(NB):
                        for q in range(groups[i]):
                            p_high(b, i, q)
                            if q == min(2, groups[i] - 1) and i + 1 == NB and not (last and k == 1):
                                for u in range(QU // 2):
                                    q_high(b + 1, u)
                        if i + 1 < NB:
                            exp(b, i + 1)
                            if i + 2 < VU:
                                v_high(b, i + 2)
                        elif not (last and k == 1):
                            for u in range(QU // 2, QU):
                                q_high(b + 1, u)
            each_pair(act, B // 2, pair)

        @block.tensor
        def _(pe):
            def queries(b, k, u):
                c, n = u % C, u // C
                if c == 0:
                    wait(pe, x_in[k][n], 16 * (b - k) + 32)
                wait(pe, exp_ok, NB * b)
                if u >= 4:
                    wait(pe, ql_ok, QU * b + u - 3)
                for d in range(C):
                    mm = split_matmuls(nc, psS[:, u % 4], keep.a_hi[:, d, c * P:(c + 1) * P], keep.a_lo[:, d, c * P:(c + 1) * P],
                                       x_hi[k][:, d, n * 512:(n + 1) * 512], x_lo[k][:, d, n * 512:(n + 1) * 512],
                                       d == 0, d == C - 1)
                mm.then_inc(q_mm, 1)

            def values(b, k, u):
                if u < 2:
                    wait(pe, ql_ok, QU * (b + 1) - 1 + u)
                else:
                    wait(pe, vl_ok, VU * b + u - 1)
                for a in range(2):
                    cols = slice((2 * u + a) * P, (2 * u + a + 1) * P)
                    for d in range(C):
                        mm = split_matmuls(nc, psS[:, 2 + u % 2, a * D:(a + 1) * D], x_hi[k][:, d, cols], x_lo[k][:, d, cols],
                                           keep.v_hi[:, d], keep.v_lo[:, d], d == 0, d == C - 1)
                mm.then_inc(v_mm, 1)

            def scores(b, k, i):
                if i == 0:
                    wait(pe, ql_ok, QU * (b + 1))
                if i == VU:
                    wait(pe, vl_ok, VU * (b + 1))
                wait(pe, exp_ok, b * NB + i)
                rows = slice(i * P, (i + 1) * P)
                for n, w in enumerate(width(i)):
                    diagonal = n == i // 4
                    for d in range(C):
                        split_matmuls(nc, psS[:, n, 0:w], q_hi[:, d, rows], q_lo[:, d, rows],
                                      x_hi[k][:, d, n * 512:n * 512 + w], x_lo[k][:, d, n * 512:n * 512 + w],
                                      d == 0, d == C - 1 and not diagonal)
                mm = nc.tensor.matmul(psS[:, i // 4, (i % 4) * P:(i % 4 + 1) * P], keep.ident_bf[:], keep.mask_bf[:],
                                      start=False, stop=True, skip_group_check=True)
                mm.then_inc(s_mm, 1)

            def transposes(b, i, q):
                n = b * TG + before[i] + q
                s = (before[i] + q) % 3
                if q == 0:
                    wait(pe, exp_ok, b * NB + i + 1)
                if before[i] + q >= 3:
                    wait(pe, pl_ok, n - 2)
                for m in range(4 * q, min(4 * q + 4, i + 1)):
                    mm = nc.tensor.transpose(psT[:, s, m % 4], prob[i % 2][:, m * P:(m + 1) * P], keep.ident[:])
                mm.then_inc(t_mm, 1)

            def weigh(b, i, q):
                n = b * TG + before[i] + q
                s = (before[i] + q) % 4
                wait(pe, pl_ok, n + 1)
                if q == 0:
                    wait(pe, o_ok, b * NB + i - 1)
                    if i < VU:
                        wait(pe, vl_ok, VU * b + i // 2 + 1)
                for m in range(4 * q, min(4 * q + 4, i + 1)):
                    mm = split_matmuls(nc, psO[:, i % 2], pT_hi[s][:, m % 4], pT_lo[s][:, m % 4],
                                       v_hi[:, m], v_lo[:, m], m == 0, m == i)
                mm.then_inc(pv_mm, 1)

            for u in range(QU):
                queries(0, 0, u)

            def pair(p, last):
                for k in range(2):
                    b = 2 * p + k
                    values(b, k, 0)
                    scores(b, k, 0)
                    values(b, k, 1)
                    for i in range(NB):
                        for q in range(min(3, groups[i])):
                            transposes(b, i, q)
                        more = not (last and k == 1)
                        if i + 1 < NB:
                            scores(b, k, i + 1)
                            if i + 2 < VU:
                                values(b, k, i + 2)
                        elif more:
                            for u in range(QU // 2):
                                queries(b + 1, 1 - k, u)
                        for q in range(groups[i]):
                            weigh(b, i, q)
                            if q + 3 < groups[i]:
                                transposes(b, i, q + 3)
                        if i + 1 == NB and more:
                            for u in range(QU // 2, QU):
                                queries(b + 1, 1 - k, u)
            each_pair(pe, B // 2, pair)


class Keep:

    def __init__(self, nc, ctx, D, E, NT, SC, ET):
        def sb(name, shape, dt):
            return ctx.enter_context(nc.sbuf_tensor("keep_" + name, shape, dt))

        C = D // P
        self.ident = sb("ident", [P, P], F32)
        self.ident_bf = sb("ident_bf", [P, P], BF16)
        self.mask_bf = sb("mask_bf", [P, P], BF16)
        self.a_hi = sb("a_hi", [P, C, D], F32R)
        self.a_lo = sb("a_lo", [P, C, D], F32R)
        self.v_hi = sb("v_hi", [P, C, D], F32R)
        self.v_lo = sb("v_lo", [P, C, D], F32R)
        self.neghalf = sb("neghalf", [P, GT // P], F32)
        self.euler = sb("euler", [P, GT // P], F32)
        self.position = sb("position", [P, NT], I32)
        self.slot_token = sb("slot_token", [P, SC], I32)
        self.tile_expert = sb("tile_expert", [1, ET + 3], I32)
        self.last_pair = sb("last_pair", [1, 1], I32)


class Ranks:

    def __init__(self, nc, ctx, E, NT):
        def sb(name, shape):
            return ctx.enter_context(nc.sbuf_tensor("ranks_" + name, shape, F32))

        self.one_hot = sb("one_hot", [P, NT, E])
        self.rank = sb("rank", [P, NT])
        self.here = sb("here", [P, E])


def build(nc, x, W_qkv, gate_w, sgw, suw, sdw, rgw, ruw, rdw, out):
    B, N, D = x.shape
    E, _, F = rgw.shape
    T = B * N
    NT, NG = T // P, T // GT
    ET = T // ST + E
    C = D // P
    x_g = x.rearrange("b n d -> (b n) d").rearrange("(g j p) d -> g p j d", p=P, j=GT // P)
    out_g = out.rearrange("b n d -> (b n) d").rearrange("(g j p) d -> g p j d", p=P, j=GT // P)
    xs = nc.dram_tensor("xs_rows", [T, D], F32).ap()
    sh = nc.dram_tensor("shared_rows", [T, D], F32).ap()
    dr = nc.dram_tensor("routed_rows", [ET * ST, D], F32).ap()
    xth = nc.dram_tensor("xT_high", [NG, P, C, GT], F32).ap()
    xtl = nc.dram_tensor("xT_low", [NG, P, C, GT], F32).ap()
    xs_g = xs.rearrange("(g j p) d -> g p j d", p=P, j=GT // P)
    sh_g = sh.rearrange("(g j p) d -> g p j d", p=P, j=GT // P)
    d_t = dr.rearrange("(t h p) d -> t p h d", p=P, h=ST // P)
    with ExitStack() as ctx:
        keep = Keep(nc, ctx, D, E, NT, (ET + 2) * ST // P, ET)
        with ExitStack() as early:
            ranks = Ranks(nc, early, E, NT)
            token_stage(nc, x_g, gate_w, sgw, suw, sdw, xs_g, xth, xtl, sh_g, keep, ranks, D, F, E, NG)
            routing_stage(nc, W_qkv, d_t, keep, ranks, D, E, NT, ET)
        expert_stage(nc, xs, rgw, ruw, rdw, d_t, keep, D, F, E, ET)
        attention_stage(nc, x_g, sh_g, dr, xth, xtl, out_g, keep, D, B, N)


_INS = ["L0_attn_x", "L0_attn_W_qkv", "L0_ffn_gate_w", "L0_ffn_shared_gate_w", "L0_ffn_shared_up_w",
        "L0_ffn_shared_down_w", "L0_ffn_routed_gate_w", "L0_ffn_routed_up_w", "L0_ffn_routed_down_w"]


def kernel(**inputs):
    import numpy as np
    from concourse import bacc
    from concourse.bass_utils import run_bass_kernel_spmd

    nc = bacc.Bacc("TRN2", target_bir_lowering=False, num_devices=1)
    arrays = {f"in_{n}": np.ascontiguousarray(inputs[n]) for n in _INS}
    args = [nc.dram_tensor(n, a.shape, mybir.dt.from_np(a.dtype), kind="ExternalInput").ap() for n, a in arrays.items()]
    out = nc.dram_tensor("out", inputs["L0_attn_x"].shape, F32, kind="ExternalOutput").ap()
    build(nc, *args, out)
    return run_bass_kernel_spmd(nc, [arrays], core_ids=[0]).results[0]["out"]
```
